# Optimizing a Trainium2 kernel written in Bass

```python
import numpy as np
import jax
import jax.numpy as jnp

def _softmax(x, axis=-1):
    return jax.nn.softmax(x, axis=axis)

def _gelu(x):
    return jax.nn.gelu(x, approximate=True)

def _silu(x):
    return jax.nn.silu(x)

def _sigmoid(x):
    return jax.nn.sigmoid(x)

def _layernorm(x, axis=-1, eps=1e-05):
    m = jnp.mean(x, axis=axis, keepdims=True)
    v = jnp.var(x, axis=axis, keepdims=True)
    return (x - m) / jnp.sqrt(v + eps)

def _scatter_add(tgt, idx, src, axis=0):
    return tgt.at[idx].add(src)

def _segment_sum(src, seg, n):
    return jax.ops.segment_sum(src, seg, n)
kernel_name = 'mk_hybrid_d1_jaxref_r4_0a09bd'

def setup_inputs(seed: int=0):
    np.random.seed(seed)
    _w = jnp.asarray

    def _L0_attn_a_setup():
        import jax, jax.numpy as jnp
        import numpy as np
        from jax import lax
        D = 256
        N = 16
        key = jax.random.key(seed)
        ks = jax.random.split(key, 8)
        sequence = jax.random.normal(ks[0], (2, 512, D), dtype=jnp.float32)
        A = jnp.broadcast_to(-jnp.arange(1, D + 1, dtype=jnp.float32)[:, None], (D, N))
        lim_B = 1.0 / np.sqrt(D)
        W_B = jax.random.uniform(ks[1], (N, D), minval=-lim_B, maxval=lim_B, dtype=jnp.float32)
        b_B = jax.random.uniform(ks[2], (N,), minval=-lim_B, maxval=lim_B, dtype=jnp.float32)
        W_C = jax.random.uniform(ks[3], (N, D), minval=-lim_B, maxval=lim_B, dtype=jnp.float32)
        b_C = jax.random.uniform(ks[4], (N,), minval=-lim_B, maxval=lim_B, dtype=jnp.float32)
        W_Delta = jax.random.uniform(ks[5], (1, D), minval=-lim_B, maxval=lim_B, dtype=jnp.float32)
        b_Delta = jax.random.uniform(ks[6], (1,), minval=-lim_B, maxval=lim_B, dtype=jnp.float32)
        u = jax.random.uniform(ks[7], (1,), dtype=jnp.float32)
        bias_Delta = jnp.log(u / (0.1 - 0.001) + 0.001)
        return {'sequence': sequence, 'A': A, 'W_B': W_B, 'b_B': b_B, 'W_C': W_C, 'b_C': b_C, 'W_Delta': W_Delta, 'b_Delta': b_Delta, 'bias_Delta': bias_Delta}
    _L0_attn_a_in = _L0_attn_a_setup()

    def _L0_attn_b_setup():
        import jax, jax.numpy as jnp
        import numpy as np
        D_MODEL = 256
        HEADS = 16
        D_K = D_MODEL // HEADS
        ROPE_BASE = 10000.0

        def _rope(x, pos_offset=0):
            S, d = (x.shape[-2], x.shape[-1])
            inv_freq = 1.0 / ROPE_BASE ** (jnp.arange(0, d, 2, dtype=jnp.float32) / d)
            pos = jnp.arange(S, dtype=jnp.float32) + pos_offset
            ang = pos[:, None] * inv_freq[None, :]
            cos, sin = (jnp.cos(ang), jnp.sin(ang))
            x1, x2 = (x[..., :d // 2], x[..., d // 2:])
            return jnp.concatenate([x1 * cos - x2 * sin, x1 * sin + x2 * cos], axis=-1)
        key = jax.random.key(seed)
        ks = jax.random.split(key, 5)
        B, S = (2, 512)
        x = jax.random.normal(ks[0], (B, S, D_MODEL), dtype=jnp.float32)
        w = lambda k: jax.random.normal(k, (D_MODEL, D_MODEL), dtype=jnp.float32) * 0.02
        z = jnp.zeros((D_MODEL,), dtype=jnp.float32)
        return {'x': x, 'Wq': w(ks[1]), 'bq': z, 'Wk': w(ks[2]), 'bk': z, 'Wv': w(ks[3]), 'bv': z, 'Wo': w(ks[4]), 'bo': z}
    _L0_attn_b_in = _L0_attn_b_setup()

    def _L0_ffn_setup():
        import jax, jax.numpy as jnp
        import numpy as np
        INPUT_SIZE = 256
        OUTPUT_SIZE = 256
        key = jax.random.key(seed)
        kx, kt, kp, ktn, kpn = jax.random.split(key, 5)
        x = jax.random.normal(kx, (8, 512, INPUT_SIZE), dtype=jnp.float32)
        theta = jax.random.normal(kt, (INPUT_SIZE, OUTPUT_SIZE), dtype=jnp.float32) * 0.02
        phi = jax.random.normal(kp, (INPUT_SIZE, OUTPUT_SIZE), dtype=jnp.float32) * 0.02
        theta_noise = jax.random.normal(ktn, (INPUT_SIZE, OUTPUT_SIZE), dtype=jnp.float32) * 0.01
        phi_noise = jax.random.normal(kpn, (INPUT_SIZE, OUTPUT_SIZE), dtype=jnp.float32) * 0.01
        return {'x': x, 'theta': theta, 'phi': phi, 'theta_noise': theta_noise, 'phi_noise': phi_noise}
    _L0_ffn_in = _L0_ffn_setup()
    _d = {'L0_attn_a_sequence': _L0_attn_a_in['sequence'], 'L0_attn_a_A': _L0_attn_a_in['A'], 'L0_attn_a_W_B': _L0_attn_a_in['W_B'], 'L0_attn_a_b_B': _L0_attn_a_in['b_B'], 'L0_attn_a_W_C': _L0_attn_a_in['W_C'], 'L0_attn_a_b_C': _L0_attn_a_in['b_C'], 'L0_attn_a_W_Delta': _L0_attn_a_in['W_Delta'], 'L0_attn_a_b_Delta': _L0_attn_a_in['b_Delta'], 'L0_attn_a_bias_Delta': _L0_attn_a_in['bias_Delta'], 'L0_attn_b_Wq': _L0_attn_b_in['Wq'], 'L0_attn_b_bq': _L0_attn_b_in['bq'], 'L0_attn_b_Wk': _L0_attn_b_in['Wk'], 'L0_attn_b_bk': _L0_attn_b_in['bk'], 'L0_attn_b_Wv': _L0_attn_b_in['Wv'], 'L0_attn_b_bv': _L0_attn_b_in['bv'], 'L0_attn_b_Wo': _L0_attn_b_in['Wo'], 'L0_attn_b_bo': _L0_attn_b_in['bo'], 'L0_ffn_theta': _L0_ffn_in['theta'], 'L0_ffn_phi': _L0_ffn_in['phi'], 'L0_ffn_theta_noise': _L0_ffn_in['theta_noise'], 'L0_ffn_phi_noise': _L0_ffn_in['phi_noise']}
    _x0 = _d['L0_attn_a_sequence']
    _d['L0_attn_a_sequence'] = jax.random.normal(jax.random.fold_in(jax.random.key(seed), 1), (1, 4096, 256), dtype=_x0.dtype)
    del _x0
    return _d

def reference(L0_attn_a_sequence, L0_attn_a_A, L0_attn_a_W_B, L0_attn_a_b_B, L0_attn_a_W_C, L0_attn_a_b_C, L0_attn_a_W_Delta, L0_attn_a_b_Delta, L0_attn_a_bias_Delta, L0_attn_b_Wq, L0_attn_b_bq, L0_attn_b_Wk, L0_attn_b_bk, L0_attn_b_Wv, L0_attn_b_bv, L0_attn_b_Wo, L0_attn_b_bo, L0_ffn_theta, L0_ffn_phi, L0_ffn_theta_noise, L0_ffn_phi_noise):

    def _L0_attn_a_ref(sequence, A, W_B, b_B, W_C, b_C, W_Delta, b_Delta, bias_Delta):
        import jax, jax.numpy as jnp
        import numpy as np
        from jax import lax
        D = 256
        N = 16
        Bm = sequence @ W_B.T + b_B
        Cm = sequence @ W_C.T + b_C
        Delta = jax.nn.softplus(sequence @ W_Delta.T + b_Delta + bias_Delta)
        A_bar = jnp.exp(A[None, None] * Delta[..., None])
        B_bar = 1.0 / A * (A_bar - 1.0) * Bm[..., None, :]

        def step(state, xs):
            Ab, Bb, x, c = xs
            state = state * Ab + x[..., None] * Bb
            y = jnp.einsum('bdn,bn->bd', state, c)
            return (state, y)
        xs = (jnp.moveaxis(A_bar, 1, 0), jnp.moveaxis(B_bar, 1, 0), jnp.moveaxis(sequence, 1, 0), jnp.moveaxis(Cm, 1, 0))
        init = jnp.zeros(sequence.shape[:-2] + (A.shape[0], A.shape[1]), dtype=sequence.dtype)
        _, ys = lax.scan(step, init, xs)
        return jnp.moveaxis(ys, 0, 1)

    def _L0_attn_b_ref(x, Wq, bq, Wk, bk, Wv, bv, Wo, bo):
        import jax, jax.numpy as jnp
        import numpy as np
        D_MODEL = 256
        HEADS = 16
        D_K = D_MODEL // HEADS
        ROPE_BASE = 10000.0

        def _rope(x, pos_offset=0):
            S, d = (x.shape[-2], x.shape[-1])
            inv_freq = 1.0 / ROPE_BASE ** (jnp.arange(0, d, 2, dtype=jnp.float32) / d)
            pos = jnp.arange(S, dtype=jnp.float32) + pos_offset
            ang = pos[:, None] * inv_freq[None, :]
            cos, sin = (jnp.cos(ang), jnp.sin(ang))
            x1, x2 = (x[..., :d // 2], x[..., d // 2:])
            return jnp.concatenate([x1 * cos - x2 * sin, x1 * sin + x2 * cos], axis=-1)
        B, S, _ = x.shape

        def split_heads(t):
            return t.reshape(B, S, HEADS, D_K).transpose(0, 2, 1, 3)
        q = split_heads(x @ Wq + bq)
        k = split_heads(x @ Wk + bk)
        v = split_heads(x @ Wv + bv)
        q = _rope(q, pos_offset=0)
        k = _rope(k, pos_offset=0)
        scores = jnp.einsum('bhqd,bhkd->bhqk', q, k) / np.sqrt(D_K).astype(np.float32)
        probs = jax.nn.softmax(scores, axis=-1)
        attn = jnp.einsum('bhqk,bhkd->bhqd', probs, v)
        out = attn.transpose(0, 2, 1, 3).reshape(B, S, D_MODEL)
        return out @ Wo + bo

    def _L0_ffn_ref(x, theta, phi, theta_noise, phi_noise):
        import jax, jax.numpy as jnp
        import numpy as np
        INPUT_SIZE = 256
        OUTPUT_SIZE = 256
        real = jnp.einsum('bti,io->bto', x, jnp.cos(theta + theta_noise))
        imag = jnp.einsum('bti,io->bto', x, jnp.sin(phi + phi_noise))
        return jnp.sqrt(real * real + imag * imag)
    x = L0_attn_a_sequence
    x = x + _L0_attn_a_ref(_layernorm(x, axis=-1), L0_attn_a_A, L0_attn_a_W_B, L0_attn_a_b_B, L0_attn_a_W_C, L0_attn_a_b_C, L0_attn_a_W_Delta, L0_attn_a_b_Delta, L0_attn_a_bias_Delta)
    x = x + _L0_ffn_ref(_layernorm(x, axis=-1), L0_ffn_theta, L0_ffn_phi, L0_ffn_theta_noise, L0_ffn_phi_noise)
    x = x + _L0_attn_b_ref(_layernorm(x, axis=-1), L0_attn_b_Wq, L0_attn_b_bq, L0_attn_b_Wk, L0_attn_b_bk, L0_attn_b_Wv, L0_attn_b_bv, L0_attn_b_Wo, L0_attn_b_bo)
    x = x + _L0_ffn_ref(_layernorm(x, axis=-1), L0_ffn_theta, L0_ffn_phi, L0_ffn_theta_noise, L0_ffn_phi_noise)
    return x

_drawn_inputs = setup_inputs


def setup_inputs(seed=0):
    import zlib

    import numpy as np

    out = dict(_drawn_inputs(seed))
    spreads = {'L0_attn_b_bq': (0.0, 0.8),
     'L0_attn_b_bk': (0.0, 0.8),
     'L0_attn_b_bv': (0.0, 0.286),
     'L0_attn_b_bo': (0.0, 0.1)}
    factors = {'L0_attn_a_b_B': 8.0,
     'L0_attn_a_b_C': 8.0,
     'L0_attn_a_W_Delta': 5.81,
     'L0_attn_b_Wq': 8.0,
     'L0_attn_b_Wk': 8.0,
     'L0_attn_b_Wv': 8.0,
     'L0_ffn_theta': 8.0,
     'L0_ffn_theta_noise': 8.0}
    for name, (base, spread) in spreads.items():
        noise = np.random.default_rng([zlib.crc32(name.encode()), seed]).standard_normal(out[name].shape)
        drawn = base * np.exp(spread * noise) if base else spread * noise
        out[name] = jnp.asarray(drawn.astype(out[name].dtype))
    for name, factor in factors.items():
        out[name] = (out[name] * factor).astype(out[name].dtype)
    return out
```

```python
from contextlib import ExitStack

import numpy as np

import concourse.bass as bass
from concourse import mybir

F32 = mybir.dt.float32
BF16 = mybir.dt.bfloat16
ACT = mybir.ActivationFunctionType
ALU = mybir.AluOpType
AXX = mybir.AxisListType.X

P = 128
S = 4096
D = 256
DH = D // P
NT = S // P
TPC = 4
CH = TPC * P
NC = S // CH
NS = 16
CPT = P // NS
NJ = D // CPT
NJH = NJ // DH
SC = 1024
NSC = S // SC
TPS = SC // P
H = 16
DK = D // H
EPS = 1e-5
NPART = 3
Q_SLOTS = (0, 0, 0, 1, 1, 2)
K_SLOTS = (0, 1, 2, 0, 1, 0)
KR = DK * len(Q_SLOTS)
KM = KR + NPART
SCALE = 0.25
QH = S // 2
NKT = S // P
STEPS = 2 * NKT
GW = 1024
VW = 32
MAXU = NT * NC
MAX_STEPS = 58
MROW_STEP = 60
TWO_PI = 2 * np.pi
C1, C2 = 6.28125, float(np.float32(TWO_PI - 6.28125))
C3 = TWO_PI - C1 - C2
ROUND = 1.5 * 2 ** 23
PI_IN = 3.1415925


class Chain:

    def __init__(self, eng, done, base=0):
        self.eng, self.done, self.base, self.n = eng, done, base, 0

    def link(self, ins):
        ins.then_inc(self.done, 1)
        self.n += 1
        self.eng.wait_ge(self.done, self.base + self.n)


class Mem:
    pass


def make_sems(nc, ctx, stage, names):
    return [ctx.enter_context(nc.semaphore(f"{stage}_{n}")) for n in names.split()]


def looped(eng, n, body):
    with eng.Fori(0, n - 1) as i:
        body(i, True)
    body(n - 1, False)


def wait_apart(eng, sem, value, passed):
    eng.wait_ge(sem, value)
    eng.sem_inc(passed, 1)


def layer_stats(nc, mem, tile):
    return nc.vector.bn_stats(mem.six[:, tile, :], mem.x[:, tile, :])


def aggregate_stats(nc, mem, done):
    for t in range(NT):
        last = nc.vector.bn_aggr(mem.mv[:, t, :], mem.six[:, t, :])
    last.then_inc(done, 1)


def norm_tiles(nc, mem, chunk, done):
    for k in range(TPC):
        t = chunk * TPC + k
        last = nc.vector.tensor_scalar(mem.xn[:, k, :], mem.x[:, t, :], mem.mv[:, t, 0:1],
                                       mem.rstd[:, t, 0:1], ALU.subtract, ALU.mult)
    last.then_inc(done, 1)


def transpose_chunk(nc, out, src, ident):
    for h in range(DH):
        for k in range(TPC):
            last = nc.tensor.transpose(out[:, h, k * P:(k + 1) * P], src[:, k, h * P:(h + 1) * P], ident[:])
    return last


def norm_and_project(nc, mem, io):
    with ExitStack() as ctx:
        def sb(name, shape, dt):
            return ctx.enter_context(nc.sbuf_tensor(name, shape, dt))

        w_bcd = sb("w_bcd", [P, DH, 3, P], F32)
        bias = sb("bias_bcd", [P, 4], F32)
        recip_a = sb("recip_a", [P, NJ], F32)
        mask = sb("channel_mask", [P, CPT], F32)
        xnt = sb("np_xnt", [P, DH, CH], F32)
        rest = sb("np_rest", [P, DH, CH], F32)
        soft = sb("np_soft", [P, S], F32)
        std = sb("np_std", [P, NT, 1], F32)
        tp = ctx.enter_context(nc.psum_tensor("np_tp", [P, DH, CH], F32))
        pb = ctx.enter_context(nc.psum_tensor("np_proj", [P, 3, CH], F32))
        (loaded, consts, pool_step, dve_step, stats_done, std_ready, gather_done, xn_ready, t_ready, xnt_ready,
         hi_ready, rest_ready, mid_ready, lo_ready, proj_ready, proj_read, neg_ready, exp_ready, ln_ready) = make_sems(
            nc, ctx, "np", "loaded consts poolstep dvestep stats std gather xn t xnt hi rest mid lo proj projread "
            "neg exp ln")
        x_loaded = make_sems(nc, ctx, "np", "x0 x1 x2 x3")

        with nc.Block() as block:
            @block.sync
            def _(sp):
                xv = io.x.rearrange("a (t p) d -> (a p) t d", p=P)
                for q in range(4):
                    sp.dma_start(mem.x[:, 8 * q:8 * q + 8, :], xv[:, 8 * q:8 * q + 8, :]).then_inc(x_loaded[q], 16)
                sp.dma_start(w_bcd[:], io.w_bcd.rearrange("(h p) j c -> p h j c", p=P)).then_inc(loaded, 16)
                sp.dma_start(bias[:], io.bias_bcd).then_inc(loaded, 16)
                sp.dma_start(mem.a_scale[:], io.a_tiles).then_inc(loaded, 16)

            @block.gpsimd
            def _(pool):
                steps = Chain(pool, pool_step)
                steps.link(nc.gpsimd.memset(mem.ident[:], 0.0))
                steps.link(nc.gpsimd.affine_select(
                    out=mem.ident[:], in_=mem.ident[:], compare_op=ALU.not_equal, fill=1.0, base=0,
                    pattern=[[-1, P]], channel_multiplier=1))
                steps.link(nc.gpsimd.tensor_copy(mem.ident_b[:], mem.ident[:]))
                steps.link(nc.gpsimd.memset(mem.spread[:], 0.0))
                v = mem.spread[:].rearrange("p j (a n) -> p j a n", n=NS)
                steps.link(nc.gpsimd.affine_select(
                    out=v, in_=v, compare_op=ALU.not_equal, fill=1.0, base=0,
                    pattern=[[-CPT, NJH], [-1, CPT], [0, NS]], channel_multiplier=1))
                steps.link(nc.gpsimd.memset(mask[:], 1.0))
                steps.link(nc.gpsimd.affine_select(out=mask[:], in_=mask[:], compare_op=ALU.is_ge, fill=0.0, base=0,
                                                   pattern=[[-NS, CPT]], channel_multiplier=1))
                steps.link(nc.gpsimd.affine_select(out=mask[:], in_=mask[:], compare_op=ALU.is_ge, fill=0.0,
                                                   base=NS - 1, pattern=[[NS, CPT]], channel_multiplier=-1))
                steps.link(nc.gpsimd.memset(mem.gather[:], 0.0))
                steps.link(nc.gpsimd.memset(mem.carry[:], 0.0))
                nc.gpsimd.memset(mem.eps[:], EPS).then_inc(consts, 1)
                with pool.Fori(0, NC) as i:
                    pool.wait_ge(hi_ready, i + 1)
                    nc.gpsimd.tensor_tensor(rest[:], xnt[:], mem.xp[:, 0, :, bass.ts(i, CH)],
                                            ALU.subtract).then_inc(rest_ready, 1)

            @block.vector
            def _(dve):
                steps = Chain(dve, dve_step)
                for q in range(4):
                    dve.wait_ge(x_loaded[q], 16)
                    for t in range(8 * q, 8 * q + 8):
                        last = layer_stats(nc, mem, t)
                steps.link(last)
                aggregate_stats(nc, mem, stats_done)
                dve.wait_ge(std_ready, 1)
                steps.link(nc.vector.reciprocal(mem.rstd[:], std[:]))
                norm_tiles(nc, mem, 0, xn_ready)
                dve.wait_ge(loaded, 48)
                dve.wait_ge(consts, 1)
                steps.link(nc.vector.reciprocal(recip_a[:], mem.a_scale[:]))
                g = mem.gather[:].rearrange("p (g r) c -> p g r c", r=4)
                ra = recip_a[:].rearrange("p (g r) -> p g r", r=4)
                for r in range(4):
                    steps.link(nc.vector.tensor_tensor(
                        g[:, :, r, CPT * r:CPT * r + CPT], mask[:].unsqueeze(1).to_broadcast([P, NJ // 4, CPT]),
                        ra[:, :, r].unsqueeze(2).to_broadcast([P, NJ // 4, CPT]), ALU.mult))
                steps.link(nc.vector.tensor_tensor(bias[:, 2:3], bias[:, 2:3], bias[:, 3:4], ALU.add))

                def chunk(i, more):
                    dve.wait_ge(t_ready, i + 1)
                    if more:
                        norm_tiles(nc, mem, i + 1, xn_ready)
                    dve.wait_ge(mid_ready, i + 1)
                    nc.vector.tensor_tensor(mem.xp[:, 2, :, bass.ts(i, CH)], rest[:], mem.xp[:, 1, :, bass.ts(i, CH)],
                                            ALU.subtract).then_inc(lo_ready, 1)
                    dve.wait_ge(proj_ready, i + 1)
                    for n, dst in enumerate((mem.b_rep, mem.c_rep, mem.delta)):
                        last = nc.vector.tensor_scalar(dst[:, bass.ts(i, CH)], pb[:, n, :], bias[:, n:n + 1], None,
                                                       ALU.add)
                    last.then_inc(proj_read, 1)

                looped(dve, NC, chunk)
                dve.wait_ge(proj_read, NC)
                nc.vector.scalar_tensor_tensor(soft[:], mem.delta[:], -1.0, mem.delta[:], ALU.mult,
                                               ALU.min).then_inc(neg_ready, 1)
                dve.wait_ge(ln_ready, 1)
                steps.link(nc.vector.scalar_tensor_tensor(mem.delta[:], mem.delta[:], 0.0, soft[:], ALU.max, ALU.add))

            @block.scalar
            def _(act):
                act.wait_ge(stats_done, 1)
                act.wait_ge(consts, 1)
                nc.scalar.activation(std[:], mem.mv[:, :, 1:2], ACT.Sqrt, bias=mem.eps[:, 0:1]).then_inc(std_ready, 1)
                act.sem_inc(lo_ready, 1)
                with act.Fori(0, NC) as i:
                    act.wait_ge(t_ready, i + 1)
                    act.wait_ge(lo_ready, i + 1)
                    nc.scalar.activation(xnt[:], tp[:], ACT.Copy).then_inc(xnt_ready, 1)
                    act.wait_ge(xnt_ready, i + 1)
                    nc.scalar.activation(mem.xp[:, 0, :, bass.ts(i, CH)], xnt[:], ACT.Copy).then_inc(hi_ready, 1)
                    act.wait_ge(rest_ready, i + 1)
                    nc.scalar.activation(mem.xp[:, 1, :, bass.ts(i, CH)], rest[:], ACT.Copy).then_inc(mid_ready, 1)
                act.wait_ge(neg_ready, 1)
                nc.scalar.activation(soft[:], soft[:], ACT.Exp).then_inc(exp_ready, 1)
                act.wait_ge(exp_ready, 1)
                nc.scalar.activation(soft[:], soft[:], ACT.Ln, bias=1.0).then_inc(ln_ready, 1)

            @block.tensor
            def _(pe):
                pe.wait_ge(consts, 1)
                pe.wait_ge(loaded, 48)
                pe.wait_ge(xn_ready, 1)
                transpose_chunk(nc, tp, mem.xn, mem.ident).then_inc(t_ready, 1)

                def chunk(i, more):
                    pe.wait_ge(xnt_ready, i + 1)
                    for n in range(3):
                        for h in range(DH):
                            last = nc.tensor.matmul(pb[:, n, :], w_bcd[:, h, n, :], xnt[:, h, :],
                                                    start=(h == 0), stop=(h == DH - 1))
                    last.then_inc(proj_ready, 1)
                    if more:
                        pe.wait_ge(xn_ready, i + 2)
                        pe.wait_ge(proj_read, i + 1)
                        transpose_chunk(nc, tp, mem.xn, mem.ident).then_inc(t_ready, 1)

                looped(pe, NC, chunk)


def selective_scan(nc, mem):
    with ExitStack() as ctx:
        def sb(name, shape, dt):
            return ctx.enter_context(nc.sbuf_tensor(name, shape, dt))

        decay = sb("decay", [P, 2, SC], F32)
        w = sb("scan_w", [P, 2, SC], F32)
        u = sb("scan_u", [P, 2, SC], F32)
        st = sb("scan_state", [P, 2, SC], F32)
        hc = sb("scan_hc", [P, 2, SC], F32)
        ysb = sb("scan_y", [P, SC], F32)
        xr = ctx.enter_context(nc.psum_tensor("x_spread", [P, 2, SC], F32))
        yb = ctx.enter_context(nc.psum_tensor("y_sum", [P, SC], F32))
        ty = ctx.enter_context(nc.psum_tensor("y_tokens", [P, TPS, P], F32))
        (xr_ready, w_done, decay_ready, u_done, scan_done, carry_saved, hc_done, y_done, y_copied, y_turned,
         x_added, act_passed, pool_passed) = make_sems(
            nc, ctx, "ss", "xr w decay u scan carry hc y ycopied yturned xadded actpassed poolpassed")

        def chunks(eng, body):
            body(0, True, False)
            with eng.Fori(1, NSC - 1) as c:
                body(c, False, False)
            body(NSC - 1, False, True)

        with nc.Block() as block:
            @block.tensor
            def _(pe):
                def spread_x(c, j, n):
                    pe.wait_ge(w_done, n + 1)
                    for b in range(SC // CH):
                        for part in range(NPART):
                            last = nc.tensor.matmul(
                                xr[:, j % 2, b * CH:(b + 1) * CH], mem.spread[:, j % NJH, :],
                                mem.xp[:, part, j // NJH, bass.ds(c * SC + b * CH, CH)],
                                start=(part == 0), stop=(part == NPART - 1))
                    last.then_inc(xr_ready, 1)

                def turn_y(k):
                    pe.wait_ge(y_copied, k)
                    pe.wait_ge(x_added, k)
                    for t in range(TPS):
                        last = nc.tensor.transpose(ty[:, t, :], ysb[:, t * P:(t + 1) * P], mem.ident[:])
                    last.then_inc(y_turned, 1)

                def chunk(c, first, last_chunk):
                    for j in range(NJ):
                        n, k, jj = c * NJ + j, c * DH + j // NJH, j % NJH
                        if j < NJ - 1:
                            spread_x(c, j + 1, n + 1)
                        elif not last_chunk:
                            spread_x(c + 1, 0, n + 1)
                        pe.wait_ge(hc_done, n + 3)
                        if jj == 0 and not (first and j == 0):
                            pe.wait_ge(y_copied, k)
                        g, r = jj // 4, jj % 4
                        for b in range(SC // CH):
                            last = nc.tensor.matmul(
                                yb[32 * g:32 * g + 32, b * CH:(b + 1) * CH], mem.gather[:, j, :],
                                hc[:, j % 2, b * CH:(b + 1) * CH], start=(r == 0), stop=(r == 3),
                                tile_position=(0, 32 * g))
                        last.then_inc(y_done, 1)
                        if jj == 2 and not (first and j < NJH):
                            turn_y(k)

                spread_x(0, 0, 0)
                chunks(pe, chunk)
                turn_y(NSC * DH)

            @block.scalar
            def _(act):
                act.sem_inc(scan_done, 2)
                act.sem_inc(y_turned, 1)

                def copy_y(k):
                    act.wait_ge(y_done, k * NJH + 2)
                    act.wait_ge(y_turned, k)
                    nc.scalar.activation(ysb[:], yb[:], ACT.Copy).then_inc(y_copied, 1)

                def chunk(c, first, last_chunk):
                    for j in range(NJ):
                        wait_apart(act, scan_done, c * NJ + j + 1, act_passed)
                        nc.scalar.activation(decay[:, j % 2, :], mem.delta[:, bass.ts(c, SC)], ACT.Exp,
                                             scale=mem.a_scale[:, j:j + 1]).then_inc(decay_ready, 1)
                        if j % NJH == 2 and not (first and j < NJH):
                            copy_y(c * DH + j // NJH)

                chunks(act, chunk)
                copy_y(NSC * DH)

            @block.vector
            def _(dve):
                dve.sem_inc(w_done, 2)
                dve.sem_inc(x_added, 1)

                def add_y(k, tile, half):
                    dve.wait_ge(y_turned, k + 1)
                    xs = mem.x[:, bass.ds(tile, TPS), half * P:(half + 1) * P]
                    nc.vector.tensor_tensor(xs, ty[:], xs, ALU.add).then_inc(x_added, 1)

                def chunk(c, first, last_chunk):
                    for j in range(NJ):
                        n, b = c * NJ + j, j % 2
                        dve.wait_ge(xr_ready, n + 1)
                        nc.vector.tensor_tensor(w[:, b, :], xr[:, b, :], mem.b_rep[:, bass.ts(c, SC)],
                                                ALU.mult).then_inc(w_done, 1)
                        dve.wait_ge(w_done, n + 3)
                        dve.wait_ge(decay_ready, n + 1)
                        nc.vector.scalar_tensor_tensor(u[:, b, :], decay[:, b, :], -1.0, w[:, b, :], ALU.add,
                                                       ALU.mult).then_inc(u_done, 1)
                        dve.wait_ge(u_done, n + 1)
                        dve.wait_ge(hc_done, n + 1)
                        dve.wait_ge(carry_saved, n + NJ - 1)
                        nc.vector.tensor_tensor_scan(st[:, b, :], decay[:, b, :], u[:, b, :], mem.carry[:, j:j + 1],
                                                     ALU.mult, ALU.add).then_inc(scan_done, 1)
                        if j % NJH == 4 and not (first and j < NJH):
                            add_y(c * DH + j // NJH, (c - 1) * TPS if j < NJH else c * TPS, 1 if j < NJH else 0)

                chunks(dve, chunk)
                add_y(NSC * DH, (NSC - 1) * TPS, 1)
                dve.wait_ge(x_added, NSC * DH + 1)
                for t in range(NT):
                    layer_stats(nc, mem, t)

            @block.gpsimd
            def _(pool):
                pool.sem_inc(carry_saved, NJ)
                pool.sem_inc(hc_done, 2)
                pool.sem_inc(y_done, 2)

                def chunk(c, first, last_chunk):
                    for j in range(NJ):
                        n, b = c * NJ + j, j % 2
                        wait_apart(pool, scan_done, n + 3, pool_passed)
                        nc.gpsimd.tensor_copy(mem.carry[:, j:j + 1], st[:, b, SC - 1:SC]).then_inc(carry_saved, 1)
                        wait_apart(pool, y_done, n + 1, pool_passed)
                        nc.gpsimd.tensor_tensor(hc[:, b, :], st[:, b, :], mem.c_rep[:, bass.ts(c, SC)],
                                                ALU.mult).then_inc(hc_done, 1)

                chunks(pool, chunk)


def ffn_weights(nc, mem, io):
    with ExitStack() as ctx:
        def sb(name, shape, dt):
            return ctx.enter_context(nc.sbuf_tensor(name, shape, dt))

        ang = sb("angle", [P, DH, 2, D], F32)
        noise = sb("angle_noise", [P, DH, 2, D], F32)
        turns = sb("angle_turns", [P, DH, 2, D], F32)
        loaded, step, ready = make_sems(nc, ctx, "fw", "loaded step ready")

        with nc.Block() as block:
            @block.sync
            def _(sp):
                for n, (w, e) in enumerate(((io.theta, io.theta_noise), (io.phi, io.phi_noise))):
                    sp.dma_start(ang[:, :, n, :], w.rearrange("(h p) o -> p h o", p=P)).then_inc(loaded, 16)
                    sp.dma_start(noise[:, :, n, :], e.rearrange("(h p) o -> p h o", p=P)).then_inc(loaded, 16)

            @block.vector
            def _(dve):
                steps = Chain(dve, step)
                dve.wait_ge(loaded, 64)
                steps.link(nc.vector.tensor_tensor(ang[:], ang[:], noise[:], ALU.add))
                steps.link(nc.vector.tensor_scalar(turns[:], ang[:], 1 / TWO_PI, None, ALU.mult))
                steps.link(nc.vector.tensor_scalar(turns[:, :, 0, :], turns[:, :, 0, :], 0.25, None, ALU.add))
                steps.link(nc.vector.tensor_scalar(turns[:], turns[:], ROUND, None, ALU.add))
                steps.link(nc.vector.tensor_scalar(turns[:], turns[:], -ROUND, None, ALU.add))
                for c in (C1, C2, C3):
                    steps.link(nc.vector.scalar_tensor_tensor(ang[:], turns[:], -c, ang[:], ALU.mult, ALU.add))
                steps.link(nc.vector.tensor_scalar(ang[:, :, 0, :], ang[:, :, 0, :], np.pi / 2, None, ALU.add))
                nc.vector.tensor_scalar(ang[:], ang[:], PI_IN, -PI_IN, ALU.min, ALU.max).then_inc(ready, 1)

            @block.scalar
            def _(act):
                act.wait_ge(ready, 1)
                nc.scalar.activation(mem.w_ffn[:], ang[:].rearrange("p h a o -> p h (a o)"), ACT.Sin)


def ffn(nc, mem, stage, out=None):
    with ExitStack() as ctx:
        xnt = ctx.enter_context(nc.sbuf_tensor(f"{stage}_xnt", [P, DH, CH], F32))
        sq = ctx.enter_context(nc.sbuf_tensor(f"{stage}_sq", [P, TPC, 2, D], F32))
        amp = ctx.enter_context(nc.sbuf_tensor(f"{stage}_amp", [P, TPC, D], F32))
        std = ctx.enter_context(nc.sbuf_tensor(f"{stage}_std", [P, NT, 1], F32))
        tp = ctx.enter_context(nc.psum_tensor(f"{stage}_tp", [P, DH, CH], F32))
        ri = ctx.enter_context(nc.psum_tensor(f"{stage}_ri", [P, TPC, 2, D], F32))
        (std_ready, rstd_ready, xn_ready, t_ready, xnt_ready, ri_ready, sq_ready, sum_ready, amp_ready, x_ready,
         stats_done, stored, dve_passed) = make_sems(
            nc, ctx, stage, "std rstd xn t xnt ri sq sum amp x stats stored passed")

        with nc.Block() as block:
            @block.scalar
            def _(act):
                act.wait_ge(stats_done, 1)
                nc.scalar.activation(std[:], mem.mv[:, :, 1:2], ACT.Sqrt, bias=mem.eps[:, 0:1]).then_inc(std_ready, 1)
                act.sem_inc(x_ready, 1)
                act.sem_inc(amp_ready, 1)
                act.wait_ge(t_ready, 1)
                nc.scalar.activation(xnt[:], tp[:], ACT.Copy).then_inc(xnt_ready, 1)

                def chunk(i, more):
                    act.wait_ge(ri_ready, i + 1)
                    act.wait_ge(amp_ready, i + 1)
                    nc.scalar.activation(sq[:], ri[:], ACT.Square).then_inc(sq_ready, 1)
                    if more:
                        act.wait_ge(t_ready, i + 2)
                        nc.scalar.activation(xnt[:], tp[:], ACT.Copy).then_inc(xnt_ready, 1)
                    act.wait_ge(sum_ready, i + 1)
                    act.wait_ge(x_ready, i + 1)
                    nc.scalar.activation(amp[:], sq[:, :, 0, :], ACT.Sqrt).then_inc(amp_ready, 1)

                looped(act, NC, chunk)

            @block.vector
            def _(dve):
                aggregate_stats(nc, mem, stats_done)
                dve.wait_ge(std_ready, 1)
                nc.vector.reciprocal(mem.rstd[:], std[:]).then_inc(rstd_ready, 1)
                dve.wait_ge(rstd_ready, 1)
                norm_tiles(nc, mem, 0, xn_ready)

                def chunk(i, more):
                    if more:
                        dve.wait_ge(t_ready, i + 1)
                        norm_tiles(nc, mem, i + 1, xn_ready)
                    dve.wait_ge(sq_ready, i + 1)
                    nc.vector.tensor_tensor(sq[:, :, 0, :], sq[:, :, 0, :], sq[:, :, 1, :],
                                            ALU.add).then_inc(sum_ready, 1)
                    dve.wait_ge(amp_ready, i + 2)
                    xs = mem.x[:, bass.ts(i, TPC), :]
                    nc.vector.tensor_tensor(xs, xs, amp[:], ALU.add).then_inc(x_ready, 1)
                    if out is None:
                        wait_apart(dve, x_ready, i + 2, dve_passed)
                        for k in range(TPC):
                            layer_stats(nc, mem, i * TPC + k)

                looped(dve, NC, chunk)

            @block.tensor
            def _(pe):
                pe.wait_ge(xn_ready, 1)
                transpose_chunk(nc, tp, mem.xn, mem.ident).then_inc(t_ready, 1)

                def chunk(i, more):
                    pe.wait_ge(xnt_ready, i + 1)
                    if more:
                        pe.wait_ge(xn_ready, i + 2)
                    for k in range(TPC):
                        for h in range(DH):
                            last = nc.tensor.matmul(ri[:, k, :, :], xnt[:, h, k * P:(k + 1) * P], mem.w_ffn[:, h, :],
                                                    start=(h == 0), stop=(h == DH - 1))
                    last.then_inc(ri_ready, 1)
                    if more:
                        transpose_chunk(nc, tp, mem.xn, mem.ident).then_inc(t_ready, 1)

                looped(pe, NC, chunk)

            if out is not None:
                @block.sync
                def _(sp):
                    ov = out.rearrange("a (t p) d -> (a p) t d", p=P)
                    with sp.Fori(0, NC) as i:
                        sp.wait_ge(x_ready, i + 2)
                        sp.dma_start(ov[:, bass.ts(i, TPC), :], mem.x[:, bass.ts(i, TPC), :]).then_inc(stored, 16)
                    sp.wait_ge(stored, 16 * NC)


def attention_project(nc, mem, io):
    with ExitStack() as ctx:
        def sb(name, shape, dt):
            return ctx.enter_context(nc.sbuf_tensor(name, shape, dt))

        w_qk = sb("w_qk", [P, 2, 2, DH, D], F32)
        b_qk = sb("b_qk", [P, 2, 2, DH], F32)
        w_v = sb("w_v", [P, DH, D], F32)
        b_v = sb("b_v", [P, D], F32)
        trig = sb("rope_trig", [P, 2, S], F32)
        xnt = sb("ap_xnt", [P, DH, CH], F32)
        std = sb("ap_std", [P, NT, 1], F32)
        term = sb("rope_terms", [P, 2, 2, CH], F32)
        roped = sb("roped", [P, 2, CH], F32)
        rest = sb("roped_rest", [P, 2, CH], F32)
        parts = sb("roped_parts", [P, 2, NPART, CH], BF16)
        tp = ctx.enter_context(nc.psum_tensor("ap_tp", [P, DH, CH], F32))
        vb = ctx.enter_context(nc.psum_tensor("ap_v", [P, TPC, D], F32))
        qb = ctx.enter_context(nc.psum_tensor("ap_qk", [P, 2, 2, CH], F32))
        (loaded, trig_loaded, std_ready, rstd_ready, xn_ready, t_ready, xnt_ready, v_ready, v_read, qk_ready, terms,
         roped_ready, hi_ready, rest_ready, mid_ready, lo_ready, stored0, stored1, stats_done) = make_sems(
            nc, ctx, "ap", "loaded trig std rstd xn t xnt v vread qk terms roped hi rest mid lo stored0 stored1 stats")
        stored = (stored0, stored1)
        NU = 2 * DH

        with nc.Block() as block:
            @block.sync
            def _(sp):
                sp.dma_start(w_v[:], io.w_v.rearrange("(h p) o -> p h o", p=P)).then_inc(loaded, 16)
                sp.dma_start(b_v[:], io.b_v).then_inc(loaded, 16)
                for a in range(2):
                    for r in range(2):
                        sp.dma_start(w_qk[:, a, r], io.w_qk[a, r].rearrange("(h p) o -> p h o", p=P)).then_inc(loaded, 16)
                sp.dma_start(b_qk[:], io.b_qk).then_inc(loaded, 16)
                sp.dma_start(trig[:], io.trig.rearrange("r p t -> p r t")).then_inc(trig_loaded, 16)
                with sp.Fori(0, NC) as i:
                    for n in range(NU):
                        a, h = n // DH, n % DH
                        sp.wait_ge(lo_ready, i * NU + n + 1)
                        sp.dma_start(mem.qk_parts[a, :, h * P:(h + 1) * P, bass.ts(i, CH)].rearrange("s p t -> p s t"),
                                     parts[:, n % 2]).then_inc(stored[n % 2], 16)
                for s in stored:
                    sp.wait_ge(s, 16 * (NC * NU // 2 + 1))

            @block.scalar
            def _(act):
                act.wait_ge(stats_done, 1)
                nc.scalar.activation(std[:], mem.mv[:, :, 1:2], ACT.Sqrt, bias=mem.eps[:, 0:1]).then_inc(std_ready, 1)
                act.sem_inc(v_read, 1)
                act.sem_inc(stored0, 16)
                act.sem_inc(stored1, 16)
                with act.Fori(0, NC) as i:
                    act.wait_ge(t_ready, i + 1)
                    nc.scalar.activation(xnt[:], tp[:], ACT.Copy).then_inc(xnt_ready, 1)
                    for n in range(NU):
                        g, b = i * NU + n, n % 2
                        act.wait_ge(roped_ready, g + 1)
                        act.wait_ge(stored[b], (i * DH + n // 2 + 1) * 16)
                        nc.scalar.activation(parts[:, b, 0], roped[:, b], ACT.Copy).then_inc(hi_ready, 1)
                        act.wait_ge(rest_ready, g + 1)
                        nc.scalar.activation(parts[:, b, 1], rest[:, b], ACT.Copy).then_inc(mid_ready, 1)

            @block.gpsimd
            def _(pool):
                with pool.Fori(0, NC) as i:
                    for n in range(NU):
                        g, b = i * NU + n, n % 2
                        pool.wait_ge(terms, g + 3)
                        nc.gpsimd.tensor_tensor(roped[:, b], term[:, b, 0], term[:, b, 1], ALU.add).then_inc(roped_ready, 1)
                        pool.wait_ge(hi_ready, g + 1)
                        nc.gpsimd.tensor_tensor(rest[:, b], roped[:, b], parts[:, b, 0],
                                                ALU.subtract).then_inc(rest_ready, 1)

            @block.vector
            def _(dve):
                dve.sem_inc(terms, 2)
                aggregate_stats(nc, mem, stats_done)
                dve.wait_ge(std_ready, 1)
                nc.vector.reciprocal(mem.rstd[:], std[:]).then_inc(rstd_ready, 1)
                dve.wait_ge(rstd_ready, 1)
                norm_tiles(nc, mem, 0, xn_ready)
                dve.wait_ge(loaded, 112)
                dve.wait_ge(trig_loaded, 16)

                def low(g, b):
                    dve.wait_ge(mid_ready, g + 1)
                    nc.vector.tensor_tensor(parts[:, b, 2], rest[:, b], parts[:, b, 1], ALU.subtract).then_inc(lo_ready, 1)

                def chunk(i, more):
                    if more:
                        dve.wait_ge(t_ready, i + 1)
                        norm_tiles(nc, mem, i + 1, xn_ready)
                    dve.wait_ge(v_ready, i + 1)
                    for k in range(TPC):
                        last = nc.vector.tensor_tensor(mem.v[:, i * TPC + k, :], vb[:, k, :], b_v[:], ALU.add)
                    last.then_inc(v_read, 1)
                    for n in range(NU):
                        a, h, g, b = n // DH, n % DH, i * NU + n, n % 2
                        dve.wait_ge(qk_ready, g + 1)
                        if n >= 2:
                            dve.wait_ge(roped_ready, g - 1)
                        for r in range(2):
                            last = nc.vector.scalar_tensor_tensor(
                                term[:, b, r], qb[:, b, r], b_qk[:, a, r, h:h + 1], trig[:, r, bass.ts(i, CH)],
                                ALU.add, ALU.mult)
                        last.then_inc(terms, 1)
                        if n:
                            low(g - 1, 1 - b)
                    low(i * NU + NU - 1, (NU - 1) % 2)

                looped(dve, NC, chunk)

            @block.tensor
            def _(pe):
                pe.wait_ge(xn_ready, 1)
                transpose_chunk(nc, tp, mem.xn, mem.ident).then_inc(t_ready, 1)
                pe.wait_ge(loaded, 112)

                def chunk(i, more):
                    pe.wait_ge(xnt_ready, i + 1)
                    pe.wait_ge(v_read, i + 1)
                    for k in range(TPC):
                        for h in range(DH):
                            last = nc.tensor.matmul(vb[:, k, :], xnt[:, h, k * P:(k + 1) * P], w_v[:, h, :],
                                                    start=(h == 0), stop=(h == DH - 1))
                    last.then_inc(v_ready, 1)
                    for n in range(NU):
                        a, half, b = n // DH, n % DH, n % 2
                        pe.wait_ge(terms, i * NU + n + 1)
                        for r in range(2):
                            for h in range(DH):
                                last = nc.tensor.matmul(qb[:, b, r, :], w_qk[:, a, r, h, half * P:(half + 1) * P],
                                                        xnt[:, h, :], start=(h == 0), stop=(h == DH - 1))
                        last.then_inc(qk_ready, 1)
                    if more:
                        pe.wait_ge(xn_ready, i + 2)
                        transpose_chunk(nc, tp, mem.xn, mem.ident).then_inc(t_ready, 1)

                looped(pe, NC, chunk)


def attention(nc, mem):
    with ExitStack() as ctx:
        def sb(name, shape, dt):
            return ctx.enter_context(nc.sbuf_tensor(name, shape, dt))

        q_rows = sb("q_rows", [P, 2, S], BF16)
        k_rows = sb("k_rows", [P, 2, S], BF16)
        v_ones = sb("v_ones", [P, 2, NKT, VW], F32)
        prob = sb("prob", [P, 2, QH], F32)
        acc_sb = sb("acc_sb", [P, CH], F32)
        rec = sb("recip_sum", [P, 4, 4, 1], F32)
        part_max = sb("part_max", [P, NT, NC], F32)
        neg_max = sb("neg_max", [P, NT], F32)
        neg_rest = sb("neg_rest", [P, NT], F32)
        neg_parts = sb("neg_parts", [P, NPART, NT], BF16)
        max_rows = sb("max_rows", [NPART * NT, P], BF16)
        sb_ = ctx.enter_context(nc.psum_tensor("scores", [P, 2, GW], F32))
        acc = ctx.enter_context(nc.psum_tensor("acc", [P, CH], F32))
        mx = ctx.enter_context(nc.psum_tensor("max_scores", [P, 2, CH], F32))
        aux = ctx.enter_context(nc.psum_tensor("aux", [P, CH], F32))
        (q_lo, k_lo, k_hi, q_hi, ones_set, v_ready, max_ready, max_read, neg_ready, aux_full, aux_read, rows_moved,
         s_ready, exp_done, pv_done, acc_read, split_step, rec_step) = make_sems(
            nc, ctx, "at", "qlo klo khi qhi ones v maxready maxread neg auxfull auxread rows s exp pv accread split rec")
        PIECE = 16 * len(Q_SLOTS)
        LO, HI = slice(0, QH), slice(QH, S)

        units = ([(t, c) for t in range(NT // 2) for c in range(NC // 2)]
                 + [(t, c) for t in range(NT // 2) for c in range(NC // 2, NC)]
                 + [(t, c) for t in range(NT // 2, NT) for c in range(NC)])

        def units_of(step):
            lo, hi = (min(MAXU, MAXU * s // MAX_STEPS) for s in (step, step + 1))
            return range(lo, hi)

        def block_use(h, half):
            if isinstance(h, int) and h == H - 1 and half == 1:
                return 3 * h + 2
            return 3 * h + 1 if half == 0 else 3 * h + 3

        def max_use(h):
            return 3 * h - 1 if not (isinstance(h, int) and h == 0) else 0

        def heads(eng, body):
            body(0, 0, True, False)
            with eng.Fori(0, (H - 2) // 2) as pair:
                body(2 * pair + 1, 1, False, False)
                body(2 * pair + 2, 0, False, False)
            body(H - 1, 1, False, True)

        with nc.Block() as block:
            @block.sync
            def _(sp):
                def load(rows, which, slots, h, par, cols, sem):
                    for n, part in enumerate(slots):
                        sp.dma_start(rows[n * DK:(n + 1) * DK, par, cols],
                                     mem.qk_parts[which, part, bass.ds(h * DK, DK), cols]).then_inc(sem, 16)

                def load_lo(h, par):
                    load(q_rows, 0, Q_SLOTS, h, par, LO, q_lo)
                    if not isinstance(h, int) or h >= 2:
                        sp.wait_ge(s_ready, (h - 2) * (2 * STEPS) + 2 * (STEPS * 3 // 4))
                    load(k_rows, 1, K_SLOTS, h, par, LO, k_lo)

                def load_hi(h, par):
                    load(k_rows, 1, K_SLOTS, h, par, HI, k_hi)
                    load(q_rows, 0, Q_SLOTS, h, par, HI, q_hi)

                def move_max(h, par):
                    sp.wait_ge(aux_read, max_use(h) + 1)
                    for n in range(NPART):
                        sp.dma_start(q_rows[KR + n:KR + n + 1, par, :].rearrange("o (t q) -> o t q", q=P),
                                     max_rows[n * NT:(n + 1) * NT, :]).then_inc(rows_moved, 16)

                def head(h, par, loads=True):
                    if loads:
                        sp.wait_ge(s_ready, h * (2 * STEPS) + STEPS)
                        load_lo(h + 2, par)
                    move_max(h + 1, 1 - par)
                    if loads:
                        sp.wait_ge(s_ready, h * (2 * STEPS) + 2 * STEPS)
                        load_hi(h + 2, par)

                load_lo(0, 0)
                load_hi(0, 0)
                sp.wait_ge(max_ready, MAXU // 2 + 1)
                load_lo(1, 1)
                load_hi(1, 1)
                move_max(0, 0)
                head(0, 0)
                with sp.Fori(0, (H - 4) // 2) as pair:
                    head(2 * pair + 1, 1)
                    head(2 * pair + 2, 0)
                head(H - 3, 1)
                head(H - 2, 0, loads=False)

            @block.gpsimd
            def _(pool):
                nc.gpsimd.memset(v_ones[:], 1.0).then_inc(ones_set, 1)
                pool.wait_ge(ones_set, 1)
                nc.gpsimd.memset(k_rows[KR:P, :, :], 1.0).then_inc(ones_set, 1)
                pool.wait_ge(ones_set, 2)

                def copy_v(h, par):
                    nc.gpsimd.tensor_copy(v_ones[:, par, :, 0:DK], mem.v[:, :, bass.ds(h * DK, DK)]).then_inc(v_ready, 1)

                copy_v(0, 0)
                copy_v(1, 1)
                with pool.Fori(0, (H - 2) // 2) as pair:
                    for par in range(2):
                        pool.wait_ge(pv_done, (2 * pair + par + 1) * STEPS)
                        copy_v(2 * pair + 2 + par, par)

            def max_unit_pe(pe, h, par, n):
                t, c = units[n]
                if n == 0:
                    pe.wait_ge(q_lo, (h + 1) * PIECE)
                    pe.wait_ge(k_lo, (h + 1) * PIECE)
                if (t, c) == (0, NC // 2):
                    pe.wait_ge(k_hi, (h + 1) * PIECE)
                if (t, c) == (NT // 2, 0):
                    pe.wait_ge(q_hi, (h + 1) * PIECE)
                u = h * MAXU + n
                if not isinstance(u, int) or u >= 2:
                    pe.wait_ge(max_read, u - 1)
                nc.tensor.matmul(mx[:, n % 2, :], q_rows[0:KR, par, t * P:(t + 1) * P],
                                 k_rows[0:KR, par, c * CH:(c + 1) * CH], start=True, stop=True).then_inc(max_ready, 1)

            def turn_max_pe(pe, h):
                use = max_use(h)
                pe.wait_ge(neg_ready, h + 1)
                if not isinstance(use, int) or use > 0:
                    pe.wait_ge(aux_read, use)
                nc.tensor.transpose(aux[:].bitcast(BF16)[0:NPART * NT, 0:P], neg_parts[:].rearrange("p s t -> p (s t)"),
                                    mem.ident_b[:]).then_inc(aux_full, 1)

            @block.tensor
            def _(pe):
                def scores(h, par, t, group):
                    half, kt = t // NKT, t % NKT
                    if t == 0 and group == 0:
                        pe.wait_ge(rows_moved, (h + 1) * 16 * NPART)
                    g = h * (2 * STEPS) + 2 * t + group
                    if not isinstance(g, int) or g >= 2:
                        pe.wait_ge(exp_done, g - 1)
                    for b in range(GW // CH):
                        q0 = half * QH + group * GW + b * CH
                        last = nc.tensor.matmul(sb_[:, group, b * CH:(b + 1) * CH],
                                                k_rows[0:KM, par, kt * P:(kt + 1) * P],
                                                q_rows[0:KM, par, q0:q0 + CH], start=True, stop=True)
                    last.then_inc(s_ready, 1)

                def turn_block(h, half):
                    pe.wait_ge(acc_read, 2 * h + half + 1)
                    pe.wait_ge(aux_read, block_use(h, half))
                    for i in range(4):
                        last = nc.tensor.transpose(aux[:, i * P:(i + 1) * P], acc_sb[:, i * P:(i + 1) * P], mem.ident[:])
                    last.then_inc(aux_full, 1)

                def head(h, par, first, last_head):
                    for t in range(STEPS):
                        half, kt = t // NKT, t % NKT
                        todo = [] if last_head else list(units_of(t))
                        for group in range(2):
                            if t < STEPS - 1:
                                scores(h, par, t + 1, group)
                            elif not last_head:
                                scores(h + 1, 1 - par, 0, group)
                            part = todo[:(len(todo) + 1) // 2] if group == 0 else todo[(len(todo) + 1) // 2:]
                            for n in part:
                                max_unit_pe(pe, h + 1, 1 - par, n)
                        if t == 0:
                            pe.wait_ge(v_ready, h + 1)
                        if kt == 0 and not (first and t == 0):
                            pe.wait_ge(acc_read, 2 * h + half)
                        pe.wait_ge(exp_done, h * (2 * STEPS) + 2 * t + 2)
                        for j in range(4):
                            last = nc.tensor.matmul(acc[32 * j:32 * j + VW, :], v_ones[:, par, kt, :],
                                                    prob[:, t % 2, j * CH:(j + 1) * CH], start=(kt == 0),
                                                    stop=(kt == NKT - 1), tile_position=(0, 32 * j))
                        last.then_inc(pv_done, 1)
                        if t == 2 and not first:
                            turn_block(h - 1, 1)
                        if t == NKT + 2:
                            turn_block(h, 0)
                        if t == MROW_STEP and not last_head:
                            turn_max_pe(pe, h + 1)

                pe.wait_ge(ones_set, 2)
                for n in range(MAXU):
                    max_unit_pe(pe, 0, 0, n)
                turn_max_pe(pe, 0)
                for group in range(2):
                    scores(0, 0, 0, group)
                heads(pe, head)
                turn_block(H - 1, 1)

            @block.scalar
            def _(act):
                def copy_block(h, half):
                    act.wait_ge(pv_done, h * STEPS + (half + 1) * NKT)
                    if half == 1:
                        act.wait_ge(aux_full, block_use(h, 0) + 1)
                    elif not isinstance(h, int) or h >= 1:
                        act.wait_ge(aux_full, block_use(h - 1, 1) + 1)
                    nc.scalar.activation(acc_sb[:], acc[:], ACT.Copy).then_inc(acc_read, 1)

                def head(h, par, first, last_head):
                    for t in range(STEPS):
                        if not (first and t < 2):
                            act.wait_ge(pv_done, h * STEPS + t - 1)
                        for group in range(2):
                            act.wait_ge(s_ready, h * (2 * STEPS) + 2 * t + group + 1)
                            nc.scalar.activation(prob[:, t % 2, group * GW:(group + 1) * GW], sb_[:, group, :], ACT.Exp,
                                                 scale=SCALE).then_inc(exp_done, 1)
                        if t == 0 and not first:
                            copy_block(h - 1, 1)
                        if t == NKT:
                            copy_block(h, 0)

                heads(act, head)
                copy_block(H - 1, 1)

            @block.vector
            def _(dve):
                def max_unit(h, n):
                    t, c = units[n]
                    dve.wait_ge(max_ready, h * MAXU + n + 1)
                    nc.vector.tensor_reduce(part_max[:, t, c:c + 1], mx[:, n % 2, :], AXX, ALU.max).then_inc(max_read, 1)

                def split_max(h):
                    dve.wait_ge(max_read, (h + 1) * MAXU)
                    steps = Chain(dve, split_step, h * 4)
                    steps.link(nc.vector.tensor_reduce(neg_max[:], part_max[:], AXX, ALU.max, negate=True))
                    steps.link(nc.vector.tensor_copy(neg_parts[:, 0, :], neg_max[:]))
                    steps.link(nc.vector.tensor_tensor(neg_rest[:], neg_max[:], neg_parts[:, 0, :], ALU.subtract))
                    steps.link(nc.vector.tensor_copy(neg_parts[:, 1, :], neg_rest[:]))
                    nc.vector.tensor_tensor(neg_parts[:, 2, :], neg_rest[:], neg_parts[:, 1, :],
                                            ALU.subtract).then_inc(neg_ready, 1)

                def copy_max(h):
                    if not isinstance(h, int) or h >= 1:
                        dve.wait_ge(rows_moved, h * 16 * NPART)
                    dve.wait_ge(aux_full, max_use(h) + 1)
                    nc.vector.tensor_copy(max_rows[:], aux[:].bitcast(BF16)[0:NPART * NT, 0:P]).then_inc(aux_read, 1)

                def normalise(h, half):
                    dve.wait_ge(aux_full, block_use(h, half) + 1)
                    blk = aux[:].rearrange("p (i j c) -> p i j c", i=4, j=4)
                    nc.vector.reciprocal(rec[:], blk[:, :, :, DK:DK + 1]).then_inc(rec_step, 1)
                    dve.wait_ge(rec_step, 2 * h + half + 1)
                    dst = mem.att[:, half * NKT // 2:(half + 1) * NKT // 2, bass.ds(h * DK, DK)]
                    nc.vector.tensor_tensor(dst.rearrange("p (j i) c -> p i j c", i=4), blk[:, :, :, 0:DK],
                                            rec[:].to_broadcast([P, 4, 4, DK]), ALU.mult).then_inc(aux_read, 1)

                def head(h, par, first, last_head):
                    for t in range(STEPS):
                        if not last_head:
                            for n in units_of(t):
                                max_unit(h + 1, n)
                        if t == MAX_STEPS - 1 and not last_head:
                            split_max(h + 1)
                        if t == 2 and not first:
                            normalise(h - 1, 1)
                        if t == NKT + 2:
                            normalise(h, 0)
                    if not last_head:
                        copy_max(h + 1)

                for n in range(MAXU):
                    max_unit(0, n)
                split_max(0)
                copy_max(0)
                heads(dve, head)
                normalise(H - 1, 1)


def attention_output(nc, mem, io):
    with ExitStack() as ctx:
        w_o = ctx.enter_context(nc.sbuf_tensor("w_o", [P, DH, D], F32))
        b_o = ctx.enter_context(nc.sbuf_tensor("b_o", [P, 1, D], F32))
        att = ctx.enter_context(nc.sbuf_tensor("att_chunk", [P, TPC, D], F32))
        att_t = ctx.enter_context(nc.sbuf_tensor("att_t", [P, DH, CH], F32))
        tp = ctx.enter_context(nc.psum_tensor("ao_tp", [P, DH, CH], F32))
        ob = ctx.enter_context(nc.psum_tensor("ao_out", [P, TPC, D], F32))
        (loaded, bias_added, att_ready, t_ready, att_t_ready, o_ready, x_ready, dve_passed) = make_sems(
            nc, ctx, "ao", "loaded bias att t attt o x passed")

        with nc.Block() as block:
            @block.sync
            def _(sp):
                sp.dma_start(w_o[:], io.w_o.rearrange("(h p) o -> p h o", p=P)).then_inc(loaded, 16)
                sp.dma_start(b_o[:, 0, :], io.b_o).then_inc(loaded, 16)

            @block.gpsimd
            def _(pool):
                pool.wait_ge(loaded, 32)
                with pool.Fori(0, NC) as i:
                    xs = mem.x[:, bass.ts(i, TPC), :]
                    nc.gpsimd.tensor_tensor(xs, xs, b_o[:].to_broadcast([P, TPC, D]), ALU.add).then_inc(bias_added, 1)

            @block.scalar
            def _(act):
                nc.scalar.activation(att[:], mem.att[:, 0:TPC, :], ACT.Copy).then_inc(att_ready, 1)

                def chunk(i, more):
                    act.wait_ge(t_ready, i + 1)
                    if more:
                        nc.scalar.activation(att[:], mem.att[:, bass.ts(i + 1, TPC), :], ACT.Copy).then_inc(att_ready, 1)
                    nc.scalar.activation(att_t[:], tp[:], ACT.Copy).then_inc(att_t_ready, 1)

                looped(act, NC, chunk)

            @block.tensor
            def _(pe):
                pe.wait_ge(loaded, 32)
                pe.sem_inc(x_ready, 1)
                with pe.Fori(0, NC) as i:
                    pe.wait_ge(att_ready, i + 1)
                    transpose_chunk(nc, tp, att, mem.ident).then_inc(t_ready, 1)
                    pe.wait_ge(att_t_ready, i + 1)
                    pe.wait_ge(x_ready, i + 1)
                    for k in range(TPC):
                        for h in range(DH):
                            last = nc.tensor.matmul(ob[:, k, :], att_t[:, h, k * P:(k + 1) * P], w_o[:, h, :],
                                                    start=(h == 0), stop=(h == DH - 1))
                    last.then_inc(o_ready, 1)

            @block.vector
            def _(dve):
                with dve.Fori(0, NC) as i:
                    dve.wait_ge(bias_added, i + 1)
                    dve.wait_ge(o_ready, i + 1)
                    xs = mem.x[:, bass.ts(i, TPC), :]
                    nc.vector.tensor_tensor(xs, ob[:], xs, ALU.add).then_inc(x_ready, 1)
                    wait_apart(dve, x_ready, i + 2, dve_passed)
                    for k in range(TPC):
                        layer_stats(nc, mem, i * TPC + k)


def hybrid_kernel(nc, io, out):
    with ExitStack() as ctx:
        def sb(name, shape, dt, where=ctx):
            return where.enter_context(nc.sbuf_tensor(name, shape, dt))

        mem = Mem()
        mem.x = sb("x_res", [P, NT, D], F32)
        mem.xn = sb("xn", [P, TPC, D], F32)
        mem.six = sb("bn_six", [P, NT, 6], F32)
        mem.mv = sb("mean_var", [P, NT, 2], F32)
        mem.rstd = sb("rstd", [P, NT, 1], F32)
        mem.ident = sb("ident", [P, P], F32)
        mem.ident_b = sb("ident_b", [P, P], BF16)
        mem.eps = sb("eps", [P, 1], F32)
        mem.w_ffn = sb("w_ffn", [P, DH, 2 * D], F32)
        with ExitStack() as scan:
            mem.xp = sb("x_parts", [P, NPART, DH, S], BF16, scan)
            mem.b_rep = sb("b_rep", [P, S], F32, scan)
            mem.c_rep = sb("c_rep", [P, S], F32, scan)
            mem.delta = sb("delta", [P, S], F32, scan)
            mem.a_scale = sb("a_scale", [P, NJ], F32, scan)
            mem.spread = sb("spread", [P, NJH, P], BF16, scan)
            mem.gather = sb("gather", [P, NJ, 32], F32, scan)
            mem.carry = sb("carry", [P, NJ], F32, scan)
            norm_and_project(nc, mem, io)
            selective_scan(nc, mem)
        ffn_weights(nc, mem, io)
        ffn(nc, mem, "f1")
        mem.qk_parts = nc.dram_tensor("qk_parts", [2, NPART, D, S], BF16, kind="Internal").ap()
        mem.v = sb("v_all", [P, NKT, D], F32)
        attention_project(nc, mem, io)
        mem.att = sb("att", [P, NT, D], F32)
        attention(nc, mem)
        attention_output(nc, mem, io)
        ffn(nc, mem, "f2", out)


def rope_tables():
    freq = (1.0 / np.float32(10000.0) ** (np.arange(0, DK, 2, dtype=np.float32) / np.float32(DK))).astype(np.float32)
    ang = (np.arange(S, dtype=np.float32)[None, :] * freq[:, None]).astype(np.float32)
    cos, sin = np.cos(ang), np.sin(ang)
    return np.stack([np.tile(np.concatenate([cos, cos]), (P // DK, 1)),
                     np.tile(np.concatenate([-sin, sin]), (P // DK, 1))]).astype(np.float32)


def kernel(**inputs):
    import concourse.bacc as bacc
    from concourse.bass_utils import run_bass_kernel_spmd

    a = {n.removeprefix("L0_"): np.asarray(v) for n, v in inputs.items()}
    heads = lambda w: w.reshape(*w.shape[:-1], H, 2, DK // 2)
    swap = lambda w: heads(w)[..., ::-1, :].reshape(w.shape)
    by_state = lambda w: np.tile(w.T, (1, CPT))
    arrays = {
        "x": a["attn_a_sequence"],
        "a_tiles": a["attn_a_A"].reshape(NJ, P).T,
        "w_bcd": np.stack([by_state(a["attn_a_W_B"]), by_state(a["attn_a_W_C"]),
                           np.tile(a["attn_a_W_Delta"].T, (1, P))], axis=1),
        "bias_bcd": np.stack([np.tile(a["attn_a_b_B"], CPT), np.tile(a["attn_a_b_C"], CPT),
                              np.tile(a["attn_a_b_Delta"], P), np.tile(a["attn_a_bias_Delta"], P)], axis=1),
        "theta": a["ffn_theta"], "theta_noise": a["ffn_theta_noise"],
        "phi": a["ffn_phi"], "phi_noise": a["ffn_phi_noise"],
        "w_qk": np.stack([np.stack([w, swap(w)]) for w in (a["attn_b_Wq"], a["attn_b_Wk"])]),
        "b_qk": np.stack([np.stack([b, swap(b)]) for b in (a["attn_b_bq"], a["attn_b_bk"])])
        .reshape(2, 2, DH, P).transpose(3, 0, 1, 2),
        "w_v": a["attn_b_Wv"], "b_v": np.tile(a["attn_b_bv"], (P, 1)),
        "w_o": a["attn_b_Wo"], "b_o": np.tile(a["attn_b_bo"], (P, 1)),
        "trig": rope_tables(),
    }
    nc = bacc.Bacc("TRN2", target_bir_lowering=False, num_devices=1)
    io = Mem()
    arrays = {f"in_{name}": np.ascontiguousarray(value) for name, value in arrays.items()}
    for name, value in arrays.items():
        io.__dict__[name.removeprefix("in_")] = nc.dram_tensor(name, value.shape, F32, kind="ExternalInput").ap()
    out = nc.dram_tensor("out", (1, S, D), F32, kind="ExternalOutput").ap()
    hybrid_kernel(nc, io, out)
    r = run_bass_kernel_spmd(nc, [arrays], core_ids=[0])
    return r.results[0]["out"]
```

```python
from contextlib import ExitStack

import numpy as np

import concourse.bass as bass
from concourse import mybir

F32 = mybir.dt.float32
BF16 = mybir.dt.bfloat16
ACT = mybir.ActivationFunctionType
ALU = mybir.AluOpType
AXX = mybir.AxisListType.X

P = 128
S = 4096
D = 256
DH = D // P
NT = S // P
TPC = 4
CH = TPC * P
NC = S // CH
NS = 16
CPT = P // NS
NJ = D // CPT
NJH = NJ // DH
SC = 1024
NSC = S // SC
TPS = SC // P
H = 16
DK = D // H
EPS = 1e-5
NPART = 3
Q_SLOTS = (0, 0, 0, 1, 1, 2)
K_SLOTS = (0, 1, 2, 0, 1, 0)
KR = DK * len(Q_SLOTS)
KM = KR + NPART
SCALE = 0.25
QH = S // 2
NKT = S // P
STEPS = 2 * NKT
SB = 3
VW = 32
MAXU = NT * NC
MAX_STEPS = 58
MROW_STEP = 60
TWO_PI = 2 * np.pi
C1, C2 = 6.28125, float(np.float32(TWO_PI - 6.28125))
C3 = TWO_PI - C1 - C2
ROUND = 1.5 * 2 ** 23
PI_IN = 3.1415925


class Chain:

    def __init__(self, eng, done, base=0):
        self.eng, self.done, self.base, self.n = eng, done, base, 0

    def link(self, ins):
        ins.then_inc(self.done, 1)
        self.n += 1
        self.eng.wait_ge(self.done, self.base + self.n)


class Mem:
    pass


def make_sems(nc, ctx, stage, names):
    return [ctx.enter_context(nc.semaphore(f"{stage}_{n}")) for n in names.split()]


def looped(eng, n, body):
    with eng.Fori(0, n - 1) as i:
        body(i, True)
    body(n - 1, False)


def wait_apart(eng, sem, value, passed):
    eng.wait_ge(sem, value)
    eng.sem_inc(passed, 1)


def layer_stats(nc, mem, tile):
    return nc.vector.bn_stats(mem.six[:, tile, :], mem.x[:, tile, :])


def aggregate_stats(nc, mem, done):
    for t in range(NT):
        last = nc.vector.bn_aggr(mem.mv[:, t, :], mem.six[:, t, :])
    last.then_inc(done, 1)


def norm_tiles(nc, mem, chunk, done):
    for k in range(TPC):
        t = chunk * TPC + k
        last = nc.vector.tensor_scalar(mem.xn[:, k, :], mem.x[:, t, :], mem.mv[:, t, 0:1],
                                       mem.rstd[:, t, 0:1], ALU.subtract, ALU.mult)
    last.then_inc(done, 1)


def transpose_chunk(nc, out, src, ident):
    for h in range(DH):
        for k in range(TPC):
            last = nc.tensor.transpose(out[:, h, k * P:(k + 1) * P], src[:, k, h * P:(h + 1) * P], ident[:])
    return last


def norm_and_project(nc, mem, io):
    with ExitStack() as ctx:
        def sb(name, shape, dt):
            return ctx.enter_context(nc.sbuf_tensor(name, shape, dt))

        w_bcd = sb("w_bcd", [P, DH, 3, P], F32)
        bias = sb("bias_bcd", [P, 4], F32)
        recip_a = sb("recip_a", [P, NJ], F32)
        mask = sb("channel_mask", [P, CPT], F32)
        xnt = sb("np_xnt", [P, DH, CH], F32)
        rest = sb("np_rest", [P, DH, CH], F32)
        soft = sb("np_soft", [P, S], F32)
        std = sb("np_std", [P, NT, 1], F32)
        tp = ctx.enter_context(nc.psum_tensor("np_tp", [P, DH, CH], F32))
        pb = ctx.enter_context(nc.psum_tensor("np_proj", [P, 3, CH], F32))
        (loaded, consts, pool_step, dve_step, stats_done, std_ready, gather_done, xn_ready, t_ready, xnt_ready,
         hi_ready, rest_ready, mid_ready, lo_ready, proj_ready, proj_read, neg_ready, exp_ready, ln_ready) = make_sems(
            nc, ctx, "np", "loaded consts poolstep dvestep stats std gather xn t xnt hi rest mid lo proj projread "
            "neg exp ln")
        x_loaded = make_sems(nc, ctx, "np", "x0 x1 x2 x3")

        with nc.Block() as block:
            @block.sync
            def _(sp):
                xv = io.x.rearrange("a (t p) d -> (a p) t d", p=P)
                for q in range(4):
                    sp.dma_start(mem.x[:, 8 * q:8 * q + 8, :], xv[:, 8 * q:8 * q + 8, :]).then_inc(x_loaded[q], 16)
                sp.dma_start(w_bcd[:], io.w_bcd.rearrange("(h p) j c -> p h j c", p=P)).then_inc(loaded, 16)
                sp.dma_start(bias[:], io.bias_bcd).then_inc(loaded, 16)
                sp.dma_start(mem.a_scale[:], io.a_tiles).then_inc(loaded, 16)

            @block.gpsimd
            def _(pool):
                steps = Chain(pool, pool_step)
                steps.link(nc.gpsimd.memset(mem.ident[:], 0.0))
                steps.link(nc.gpsimd.affine_select(
                    out=mem.ident[:], in_=mem.ident[:], compare_op=ALU.not_equal, fill=1.0, base=0,
                    pattern=[[-1, P]], channel_multiplier=1))
                steps.link(nc.gpsimd.tensor_copy(mem.ident_b[:], mem.ident[:]))
                steps.link(nc.gpsimd.memset(mem.spread[:], 0.0))
                v = mem.spread[:].rearrange("p j (a n) -> p j a n", n=NS)
                steps.link(nc.gpsimd.affine_select(
                    out=v, in_=v, compare_op=ALU.not_equal, fill=1.0, base=0,
                    pattern=[[-CPT, NJH], [-1, CPT], [0, NS]], channel_multiplier=1))
                steps.link(nc.gpsimd.memset(mask[:], 1.0))
                steps.link(nc.gpsimd.affine_select(out=mask[:], in_=mask[:], compare_op=ALU.is_ge, fill=0.0, base=0,
                                                   pattern=[[-NS, CPT]], channel_multiplier=1))
                steps.link(nc.gpsimd.affine_select(out=mask[:], in_=mask[:], compare_op=ALU.is_ge, fill=0.0,
                                                   base=NS - 1, pattern=[[NS, CPT]], channel_multiplier=-1))
                steps.link(nc.gpsimd.memset(mem.gather[:], 0.0))
                steps.link(nc.gpsimd.memset(mem.carry[:], 0.0))
                nc.gpsimd.memset(mem.eps[:], EPS).then_inc(consts, 1)
                with pool.Fori(0, NC) as i:
                    pool.wait_ge(hi_ready, i + 1)
                    nc.gpsimd.tensor_tensor(rest[:], xnt[:], mem.xp[:, 0, :, bass.ts(i, CH)],
                                            ALU.subtract).then_inc(rest_ready, 1)

            @block.vector
            def _(dve):
                steps = Chain(dve, dve_step)
                for q in range(4):
                    dve.wait_ge(x_loaded[q], 16)
                    for t in range(8 * q, 8 * q + 8):
                        last = layer_stats(nc, mem, t)
                steps.link(last)
                aggregate_stats(nc, mem, stats_done)
                dve.wait_ge(std_ready, 1)
                steps.link(nc.vector.reciprocal(mem.rstd[:], std[:]))
                norm_tiles(nc, mem, 0, xn_ready)
                dve.wait_ge(loaded, 48)
                dve.wait_ge(consts, 1)
                steps.link(nc.vector.reciprocal(recip_a[:], mem.a_scale[:]))
                g = mem.gather[:].rearrange("p (g r) c -> p g r c", r=4)
                ra = recip_a[:].rearrange("p (g r) -> p g r", r=4)
                for r in range(4):
                    steps.link(nc.vector.tensor_tensor(
                        g[:, :, r, CPT * r:CPT * r + CPT], mask[:].unsqueeze(1).to_broadcast([P, NJ // 4, CPT]),
                        ra[:, :, r].unsqueeze(2).to_broadcast([P, NJ // 4, CPT]), ALU.mult))
                steps.link(nc.vector.tensor_tensor(bias[:, 2:3], bias[:, 2:3], bias[:, 3:4], ALU.add))

                def chunk(i, more):
                    dve.wait_ge(t_ready, i + 1)
                    if more:
                        norm_tiles(nc, mem, i + 1, xn_ready)
                    dve.wait_ge(mid_ready, i + 1)
                    nc.vector.tensor_tensor(mem.xp[:, 2, :, bass.ts(i, CH)], rest[:], mem.xp[:, 1, :, bass.ts(i, CH)],
                                            ALU.subtract).then_inc(lo_ready, 1)
                    dve.wait_ge(proj_ready, i + 1)
                    for n, dst in enumerate((mem.b_rep, mem.c_rep, mem.delta)):
                        last = nc.vector.tensor_scalar(dst[:, bass.ts(i, CH)], pb[:, n, :], bias[:, n:n + 1], None,
                                                       ALU.add)
                    last.then_inc(proj_read, 1)

                looped(dve, NC, chunk)
                dve.wait_ge(proj_read, NC)
                nc.vector.scalar_tensor_tensor(soft[:], mem.delta[:], -1.0, mem.delta[:], ALU.mult,
                                               ALU.min).then_inc(neg_ready, 1)
                dve.wait_ge(ln_ready, 1)
                steps.link(nc.vector.scalar_tensor_tensor(mem.delta[:], mem.delta[:], 0.0, soft[:], ALU.max, ALU.add))

            @block.scalar
            def _(act):
                act.wait_ge(stats_done, 1)
                act.wait_ge(consts, 1)
                nc.scalar.activation(std[:], mem.mv[:, :, 1:2], ACT.Sqrt, bias=mem.eps[:, 0:1]).then_inc(std_ready, 1)
                act.sem_inc(lo_ready, 1)
                with act.Fori(0, NC) as i:
                    act.wait_ge(t_ready, i + 1)
                    act.wait_ge(lo_ready, i + 1)
                    nc.scalar.activation(xnt[:], tp[:], ACT.Copy).then_inc(xnt_ready, 1)
                    act.wait_ge(xnt_ready, i + 1)
                    nc.scalar.activation(mem.xp[:, 0, :, bass.ts(i, CH)], xnt[:], ACT.Copy).then_inc(hi_ready, 1)
                    act.wait_ge(rest_ready, i + 1)
                    nc.scalar.activation(mem.xp[:, 1, :, bass.ts(i, CH)], rest[:], ACT.Copy).then_inc(mid_ready, 1)
                act.wait_ge(neg_ready, 1)
                nc.scalar.activation(soft[:], soft[:], ACT.Exp).then_inc(exp_ready, 1)
                act.wait_ge(exp_ready, 1)
                nc.scalar.activation(soft[:], soft[:], ACT.Ln, bias=1.0).then_inc(ln_ready, 1)

            @block.tensor
            def _(pe):
                pe.wait_ge(consts, 1)
                pe.wait_ge(loaded, 48)
                pe.wait_ge(xn_ready, 1)
                transpose_chunk(nc, tp, mem.xn, mem.ident).then_inc(t_ready, 1)

                def chunk(i, more):
                    pe.wait_ge(xnt_ready, i + 1)
                    for n in range(3):
                        for h in range(DH):
                            last = nc.tensor.matmul(pb[:, n, :], w_bcd[:, h, n, :], xnt[:, h, :],
                                                    start=(h == 0), stop=(h == DH - 1))
                    last.then_inc(proj_ready, 1)
                    if more:
                        pe.wait_ge(xn_ready, i + 2)
                        pe.wait_ge(proj_read, i + 1)
                        transpose_chunk(nc, tp, mem.xn, mem.ident).then_inc(t_ready, 1)

                looped(pe, NC, chunk)


def selective_scan(nc, mem):
    with ExitStack() as ctx:
        def sb(name, shape, dt):
            return ctx.enter_context(nc.sbuf_tensor(name, shape, dt))

        decay = sb("decay", [P, 2, SC], F32)
        w = sb("scan_w", [P, 2, SC], F32)
        u = sb("scan_u", [P, 2, SC], F32)
        st = sb("scan_state", [P, 2, SC], F32)
        hc = sb("scan_hc", [P, 2, SC], F32)
        ysb = sb("scan_y", [P, SC], F32)
        xr = ctx.enter_context(nc.psum_tensor("x_spread", [P, 2, SC], F32))
        yb = ctx.enter_context(nc.psum_tensor("y_sum", [P, SC], F32))
        ty = ctx.enter_context(nc.psum_tensor("y_tokens", [P, TPS, P], F32))
        (xr_ready, w_done, decay_ready, u_done, scan_done, carry_saved, hc_done, y_done, y_copied, y_turned,
         x_added, act_passed, pool_passed) = make_sems(
            nc, ctx, "ss", "xr w decay u scan carry hc y ycopied yturned xadded actpassed poolpassed")

        def chunks(eng, body):
            body(0, True, False)
            with eng.Fori(1, NSC - 1) as c:
                body(c, False, False)
            body(NSC - 1, False, True)

        with nc.Block() as block:
            @block.tensor
            def _(pe):
                def spread_x(c, j, n):
                    pe.wait_ge(w_done, n + 1)
                    for b in range(SC // CH):
                        for part in range(NPART):
                            last = nc.tensor.matmul(
                                xr[:, j % 2, b * CH:(b + 1) * CH], mem.spread[:, j % NJH, :],
                                mem.xp[:, part, j // NJH, bass.ds(c * SC + b * CH, CH)],
                                start=(part == 0), stop=(part == NPART - 1))
                    last.then_inc(xr_ready, 1)

                def turn_y(k):
                    pe.wait_ge(y_copied, k)
                    pe.wait_ge(x_added, k)
                    for t in range(TPS):
                        last = nc.tensor.transpose(ty[:, t, :], ysb[:, t * P:(t + 1) * P], mem.ident[:])
                    last.then_inc(y_turned, 1)

                def chunk(c, first, last_chunk):
                    for j in range(NJ):
                        n, k, jj = c * NJ + j, c * DH + j // NJH, j % NJH
                        if j < NJ - 2:
                            spread_x(c, j + 2, n + 2)
                        elif not last_chunk:
                            spread_x(c + 1, j + 2 - NJ, n + 2)
                        pe.wait_ge(hc_done, n + 3)
                        if jj == 0 and not (first and j == 0):
                            pe.wait_ge(y_copied, k)
                        g, r = jj // 4, jj % 4
                        for b in range(SC // CH):
                            last = nc.tensor.matmul(
                                yb[32 * g:32 * g + 32, b * CH:(b + 1) * CH], mem.gather[:, j, :],
                                hc[:, j % 2, b * CH:(b + 1) * CH], start=(r == 0), stop=(r == 3),
                                tile_position=(0, 32 * g))
                        last.then_inc(y_done, 1)
                        if jj == 2 and not (first and j < NJH):
                            turn_y(k)

                spread_x(0, 0, 0)
                spread_x(0, 1, 1)
                chunks(pe, chunk)
                turn_y(NSC * DH)

            @block.scalar
            def _(act):
                act.sem_inc(scan_done, 2)
                act.sem_inc(y_turned, 1)

                def copy_y(k):
                    act.wait_ge(y_done, k * NJH + 2)
                    act.wait_ge(y_turned, k)
                    nc.scalar.activation(ysb[:], yb[:], ACT.Copy).then_inc(y_copied, 1)

                def chunk(c, first, last_chunk):
                    for j in range(NJ):
                        wait_apart(act, scan_done, c * NJ + j + 1, act_passed)
                        nc.scalar.activation(decay[:, j % 2, :], mem.delta[:, bass.ts(c, SC)], ACT.Exp,
                                             scale=mem.a_scale[:, j:j + 1]).then_inc(decay_ready, 1)
                        if j % NJH == 2 and not (first and j < NJH):
                            copy_y(c * DH + j // NJH)

                chunks(act, chunk)
                copy_y(NSC * DH)

            @block.vector
            def _(dve):
                dve.sem_inc(w_done, 2)
                dve.sem_inc(x_added, 1)

                def add_y(k, tile, half):
                    dve.wait_ge(y_turned, k + 1)
                    xs = mem.x[:, bass.ds(tile, TPS), half * P:(half + 1) * P]
                    nc.vector.tensor_tensor(xs, ty[:], xs, ALU.add).then_inc(x_added, 1)

                def chunk(c, first, last_chunk):
                    for j in range(NJ):
                        n, b = c * NJ + j, j % 2
                        dve.wait_ge(xr_ready, n + 1)
                        nc.vector.tensor_tensor(w[:, b, :], xr[:, b, :], mem.b_rep[:, bass.ts(c, SC)],
                                                ALU.mult).then_inc(w_done, 1)
                        dve.wait_ge(w_done, n + 3)
                        dve.wait_ge(decay_ready, n + 1)
                        nc.vector.scalar_tensor_tensor(u[:, b, :], decay[:, b, :], -1.0, w[:, b, :], ALU.add,
                                                       ALU.mult).then_inc(u_done, 1)
                        dve.wait_ge(u_done, n + 1)
                        dve.wait_ge(hc_done, n + 1)
                        dve.wait_ge(carry_saved, n + NJ - 1)
                        nc.vector.tensor_tensor_scan(st[:, b, :], decay[:, b, :], u[:, b, :], mem.carry[:, j:j + 1],
                                                     ALU.mult, ALU.add).then_inc(scan_done, 1)
                        if j % NJH == 4 and not (first and j < NJH):
                            add_y(c * DH + j // NJH, (c - 1) * TPS if j < NJH else c * TPS, 1 if j < NJH else 0)

                chunks(dve, chunk)
                add_y(NSC * DH, (NSC - 1) * TPS, 1)
                dve.wait_ge(x_added, NSC * DH + 1)
                for t in range(NT):
                    layer_stats(nc, mem, t)

            @block.gpsimd
            def _(pool):
                pool.sem_inc(carry_saved, NJ)
                pool.sem_inc(hc_done, 2)
                pool.sem_inc(y_done, 2)

                def chunk(c, first, last_chunk):
                    for j in range(NJ):
                        n, b = c * NJ + j, j % 2
                        wait_apart(pool, scan_done, n + 3, pool_passed)
                        nc.gpsimd.tensor_copy(mem.carry[:, j:j + 1], st[:, b, SC - 1:SC]).then_inc(carry_saved, 1)
                        wait_apart(pool, y_done, n + 1, pool_passed)
                        nc.gpsimd.tensor_tensor(hc[:, b, :], st[:, b, :], mem.c_rep[:, bass.ts(c, SC)],
                                                ALU.mult).then_inc(hc_done, 1)

                chunks(pool, chunk)


def ffn_weights(nc, mem, io):
    with ExitStack() as ctx:
        def sb(name, shape, dt):
            return ctx.enter_context(nc.sbuf_tensor(name, shape, dt))

        ang = sb("angle", [P, DH, 2, D], F32)
        noise = sb("angle_noise", [P, DH, 2, D], F32)
        turns = sb("angle_turns", [P, DH, 2, D], F32)
        loaded, step, ready = make_sems(nc, ctx, "fw", "loaded step ready")

        with nc.Block() as block:
            @block.sync
            def _(sp):
                for n, (w, e) in enumerate(((io.theta, io.theta_noise), (io.phi, io.phi_noise))):
                    sp.dma_start(ang[:, :, n, :], w.rearrange("(h p) o -> p h o", p=P)).then_inc(loaded, 16)
                    sp.dma_start(noise[:, :, n, :], e.rearrange("(h p) o -> p h o", p=P)).then_inc(loaded, 16)

            @block.vector
            def _(dve):
                steps = Chain(dve, step)
                dve.wait_ge(loaded, 64)
                steps.link(nc.vector.tensor_tensor(ang[:], ang[:], noise[:], ALU.add))
                steps.link(nc.vector.tensor_scalar(turns[:], ang[:], 1 / TWO_PI, None, ALU.mult))
                steps.link(nc.vector.tensor_scalar(turns[:, :, 0, :], turns[:, :, 0, :], 0.25, None, ALU.add))
                steps.link(nc.vector.tensor_scalar(turns[:], turns[:], ROUND, None, ALU.add))
                steps.link(nc.vector.tensor_scalar(turns[:], turns[:], -ROUND, None, ALU.add))
                for c in (C1, C2, C3):
                    steps.link(nc.vector.scalar_tensor_tensor(ang[:], turns[:], -c, ang[:], ALU.mult, ALU.add))
                steps.link(nc.vector.tensor_scalar(ang[:, :, 0, :], ang[:, :, 0, :], np.pi / 2, None, ALU.add))
                nc.vector.tensor_scalar(ang[:], ang[:], PI_IN, -PI_IN, ALU.min, ALU.max).then_inc(ready, 1)

            @block.scalar
            def _(act):
                act.wait_ge(ready, 1)
                nc.scalar.activation(mem.w_ffn[:], ang[:].rearrange("p h a o -> p h (a o)"), ACT.Sin)


def ffn(nc, mem, stage, out=None):
    with ExitStack() as ctx:
        xnt = ctx.enter_context(nc.sbuf_tensor(f"{stage}_xnt", [P, DH, CH], F32))
        sq = ctx.enter_context(nc.sbuf_tensor(f"{stage}_sq", [P, TPC, 2, D], F32))
        amp = ctx.enter_context(nc.sbuf_tensor(f"{stage}_amp", [P, TPC, D], F32))
        std = ctx.enter_context(nc.sbuf_tensor(f"{stage}_std", [P, NT, 1], F32))
        tp = ctx.enter_context(nc.psum_tensor(f"{stage}_tp", [P, DH, CH], F32))
        ri = ctx.enter_context(nc.psum_tensor(f"{stage}_ri", [P, TPC, 2, D], F32))
        (std_ready, rstd_ready, xn_ready, t_ready, xnt_ready, ri_ready, sq_ready, sum_ready, amp_ready, x_ready,
         stats_done, stored, dve_passed) = make_sems(
            nc, ctx, stage, "std rstd xn t xnt ri sq sum amp x stats stored passed")

        with nc.Block() as block:
            @block.scalar
            def _(act):
                act.wait_ge(stats_done, 1)
                nc.scalar.activation(std[:], mem.mv[:, :, 1:2], ACT.Sqrt, bias=mem.eps[:, 0:1]).then_inc(std_ready, 1)
                act.sem_inc(x_ready, 1)
                act.sem_inc(amp_ready, 1)
                act.wait_ge(t_ready, 1)
                nc.scalar.activation(xnt[:], tp[:], ACT.Copy).then_inc(xnt_ready, 1)

                def chunk(i, more):
                    act.wait_ge(ri_ready, i + 1)
                    act.wait_ge(amp_ready, i + 1)
                    nc.scalar.activation(sq[:], ri[:], ACT.Square).then_inc(sq_ready, 1)
                    if more:
                        act.wait_ge(t_ready, i + 2)
                        nc.scalar.activation(xnt[:], tp[:], ACT.Copy).then_inc(xnt_ready, 1)
                    act.wait_ge(sum_ready, i + 1)
                    act.wait_ge(x_ready, i + 1)
                    nc.scalar.activation(amp[:], sq[:, :, 0, :], ACT.Sqrt).then_inc(amp_ready, 1)

                looped(act, NC, chunk)

            @block.vector
            def _(dve):
                aggregate_stats(nc, mem, stats_done)
                dve.wait_ge(std_ready, 1)
                nc.vector.reciprocal(mem.rstd[:], std[:]).then_inc(rstd_ready, 1)
                dve.wait_ge(rstd_ready, 1)
                norm_tiles(nc, mem, 0, xn_ready)

                def chunk(i, more):
                    if more:
                        dve.wait_ge(t_ready, i + 1)
                        norm_tiles(nc, mem, i + 1, xn_ready)
                    dve.wait_ge(sq_ready, i + 1)
                    nc.vector.tensor_tensor(sq[:, :, 0, :], sq[:, :, 0, :], sq[:, :, 1, :],
                                            ALU.add).then_inc(sum_ready, 1)
                    dve.wait_ge(amp_ready, i + 2)
                    xs = mem.x[:, bass.ts(i, TPC), :]
                    nc.vector.tensor_tensor(xs, xs, amp[:], ALU.add).then_inc(x_ready, 1)
                    if out is None:
                        wait_apart(dve, x_ready, i + 2, dve_passed)
                        for k in range(TPC):
                            layer_stats(nc, mem, i * TPC + k)

                looped(dve, NC, chunk)

            @block.tensor
            def _(pe):
                pe.wait_ge(xn_ready, 1)
                transpose_chunk(nc, tp, mem.xn, mem.ident).then_inc(t_ready, 1)

                def chunk(i, more):
                    pe.wait_ge(xnt_ready, i + 1)
                    if more:
                        pe.wait_ge(xn_ready, i + 2)
                    for k in range(TPC):
                        for h in range(DH):
                            last = nc.tensor.matmul(ri[:, k, :, :], xnt[:, h, k * P:(k + 1) * P], mem.w_ffn[:, h, :],
                                                    start=(h == 0), stop=(h == DH - 1))
                    last.then_inc(ri_ready, 1)
                    if more:
                        transpose_chunk(nc, tp, mem.xn, mem.ident).then_inc(t_ready, 1)

                looped(pe, NC, chunk)

            if out is not None:
                @block.sync
                def _(sp):
                    ov = out.rearrange("a (t p) d -> (a p) t d", p=P)
                    with sp.Fori(0, NC) as i:
                        sp.wait_ge(x_ready, i + 2)
                        sp.dma_start(ov[:, bass.ts(i, TPC), :], mem.x[:, bass.ts(i, TPC), :]).then_inc(stored, 16)
                    sp.wait_ge(stored, 16 * NC)


def attention_project(nc, mem, io):
    with ExitStack() as ctx:
        def sb(name, shape, dt):
            return ctx.enter_context(nc.sbuf_tensor(name, shape, dt))

        w_qk = sb("w_qk", [P, 2, 2, DH, D], F32)
        b_qk = sb("b_qk", [P, 2, 2, DH], F32)
        w_v = sb("w_v", [P, DH, D], F32)
        b_v = sb("b_v", [P, D], F32)
        trig = sb("rope_trig", [P, 2, S], F32)
        xnt = sb("ap_xnt", [P, DH, CH], F32)
        std = sb("ap_std", [P, NT, 1], F32)
        term = sb("rope_terms", [P, 2, 2, CH], F32)
        roped = sb("roped", [P, 2, CH], F32)
        rest = sb("roped_rest", [P, 2, CH], F32)
        parts = sb("roped_parts", [P, 2, NPART, CH], BF16)
        tp = ctx.enter_context(nc.psum_tensor("ap_tp", [P, DH, CH], F32))
        vb = ctx.enter_context(nc.psum_tensor("ap_v", [P, TPC, D], F32))
        qb = ctx.enter_context(nc.psum_tensor("ap_qk", [P, 2, 2, CH], F32))
        (loaded, trig_loaded, std_ready, rstd_ready, xn_ready, t_ready, xnt_ready, v_ready, v_read, qk_ready, terms,
         roped_ready, hi_ready, rest_ready, mid_ready, lo_ready, stored0, stored1, stats_done) = make_sems(
            nc, ctx, "ap", "loaded trig std rstd xn t xnt v vread qk terms roped hi rest mid lo stored0 stored1 stats")
        stored = (stored0, stored1)
        NU = 2 * DH

        with nc.Block() as block:
            @block.sync
            def _(sp):
                sp.dma_start(w_v[:], io.w_v.rearrange("(h p) o -> p h o", p=P)).then_inc(loaded, 16)
                sp.dma_start(b_v[:], io.b_v).then_inc(loaded, 16)
                for a in range(2):
                    for r in range(2):
                        sp.dma_start(w_qk[:, a, r], io.w_qk[a, r].rearrange("(h p) o -> p h o", p=P)).then_inc(loaded, 16)
                sp.dma_start(b_qk[:], io.b_qk).then_inc(loaded, 16)
                sp.dma_start(trig[:], io.trig.rearrange("r p t -> p r t")).then_inc(trig_loaded, 16)
                with sp.Fori(0, NC) as i:
                    for n in range(NU):
                        a, h = n // DH, n % DH
                        sp.wait_ge(lo_ready, i * NU + n + 1)
                        sp.dma_start(mem.qk_parts[a, :, h * P:(h + 1) * P, bass.ts(i, CH)].rearrange("s p t -> p s t"),
                                     parts[:, n % 2]).then_inc(stored[n % 2], 16)
                for s in stored:
                    sp.wait_ge(s, 16 * (NC * NU // 2 + 1))

            @block.scalar
            def _(act):
                act.wait_ge(stats_done, 1)
                nc.scalar.activation(std[:], mem.mv[:, :, 1:2], ACT.Sqrt, bias=mem.eps[:, 0:1]).then_inc(std_ready, 1)
                act.sem_inc(v_read, 1)
                act.sem_inc(stored0, 16)
                act.sem_inc(stored1, 16)
                with act.Fori(0, NC) as i:
                    act.wait_ge(t_ready, i + 1)
                    nc.scalar.activation(xnt[:], tp[:], ACT.Copy).then_inc(xnt_ready, 1)
                    for n in range(NU):
                        g, b = i * NU + n, n % 2
                        act.wait_ge(roped_ready, g + 1)
                        act.wait_ge(stored[b], (i * DH + n // 2 + 1) * 16)
                        nc.scalar.activation(parts[:, b, 0], roped[:, b], ACT.Copy).then_inc(hi_ready, 1)
                        act.wait_ge(rest_ready, g + 1)
                        nc.scalar.activation(parts[:, b, 1], rest[:, b], ACT.Copy).then_inc(mid_ready, 1)

            @block.gpsimd
            def _(pool):
                with pool.Fori(0, NC) as i:
                    for n in range(NU):
                        g, b = i * NU + n, n % 2
                        pool.wait_ge(terms, g + 3)
                        nc.gpsimd.tensor_tensor(roped[:, b], term[:, b, 0], term[:, b, 1], ALU.add).then_inc(roped_ready, 1)
                        pool.wait_ge(hi_ready, g + 1)
                        nc.gpsimd.tensor_tensor(rest[:, b], roped[:, b], parts[:, b, 0],
                                                ALU.subtract).then_inc(rest_ready, 1)

            @block.vector
            def _(dve):
                dve.sem_inc(terms, 2)
                aggregate_stats(nc, mem, stats_done)
                dve.wait_ge(std_ready, 1)
                nc.vector.reciprocal(mem.rstd[:], std[:]).then_inc(rstd_ready, 1)
                dve.wait_ge(rstd_ready, 1)
                norm_tiles(nc, mem, 0, xn_ready)
                dve.wait_ge(loaded, 112)
                dve.wait_ge(trig_loaded, 16)

                def low(g, b):
                    dve.wait_ge(mid_ready, g + 1)
                    nc.vector.tensor_tensor(parts[:, b, 2], rest[:, b], parts[:, b, 1], ALU.subtract).then_inc(lo_ready, 1)

                def chunk(i, more):
                    if more:
                        dve.wait_ge(t_ready, i + 1)
                        norm_tiles(nc, mem, i + 1, xn_ready)
                    dve.wait_ge(v_ready, i + 1)
                    for k in range(TPC):
                        last = nc.vector.tensor_tensor(mem.v[:, i * TPC + k, :], vb[:, k, :], b_v[:], ALU.add)
                    last.then_inc(v_read, 1)
                    for n in range(NU):
                        a, h, g, b = n // DH, n % DH, i * NU + n, n % 2
                        dve.wait_ge(qk_ready, g + 1)
                        if n >= 2:
                            dve.wait_ge(roped_ready, g - 1)
                        for r in range(2):
                            last = nc.vector.scalar_tensor_tensor(
                                term[:, b, r], qb[:, b, r], b_qk[:, a, r, h:h + 1], trig[:, r, bass.ts(i, CH)],
                                ALU.add, ALU.mult)
                        last.then_inc(terms, 1)
                        if n:
                            low(g - 1, 1 - b)
                    low(i * NU + NU - 1, (NU - 1) % 2)

                looped(dve, NC, chunk)

            @block.tensor
            def _(pe):
                pe.wait_ge(xn_ready, 1)
                transpose_chunk(nc, tp, mem.xn, mem.ident).then_inc(t_ready, 1)
                pe.wait_ge(loaded, 112)

                def chunk(i, more):
                    pe.wait_ge(xnt_ready, i + 1)
                    pe.wait_ge(v_read, i + 1)
                    for k in range(TPC):
                        for h in range(DH):
                            last = nc.tensor.matmul(vb[:, k, :], xnt[:, h, k * P:(k + 1) * P], w_v[:, h, :],
                                                    start=(h == 0), stop=(h == DH - 1))
                    last.then_inc(v_ready, 1)
                    for n in range(NU):
                        a, half, b = n // DH, n % DH, n % 2
                        pe.wait_ge(terms, i * NU + n + 1)
                        for r in range(2):
                            for h in range(DH):
                                last = nc.tensor.matmul(qb[:, b, r, :], w_qk[:, a, r, h, half * P:(half + 1) * P],
                                                        xnt[:, h, :], start=(h == 0), stop=(h == DH - 1))
                        last.then_inc(qk_ready, 1)
                    if more:
                        pe.wait_ge(xn_ready, i + 2)
                        transpose_chunk(nc, tp, mem.xn, mem.ident).then_inc(t_ready, 1)

                looped(pe, NC, chunk)


def attention(nc, mem):
    with ExitStack() as ctx:
        def sb(name, shape, dt):
            return ctx.enter_context(nc.sbuf_tensor(name, shape, dt))

        q_rows = sb("q_rows", [P, 2, S], BF16)
        k_rows = sb("k_rows", [P, 2, S], BF16)
        v_ones = sb("v_ones", [P, 2, NKT, VW], F32)
        prob = sb("prob", [P, 2, QH], F32)
        acc_sb = sb("acc_sb", [P, 2, CH], F32)
        part_max = sb("part_max", [P, NT, NC], F32)
        neg_max = sb("neg_max", [P, NT], F32)
        neg_rest = sb("neg_rest", [P, NT], F32)
        neg_parts = sb("neg_parts", [P, NPART, NT], BF16)
        max_rows = sb("max_rows", [NPART * NT, P], BF16)
        sc = ctx.enter_context(nc.psum_tensor("scores", [P, SB, CH], F32))
        acc = ctx.enter_context(nc.psum_tensor("acc", [P, CH], F32))
        mx = ctx.enter_context(nc.psum_tensor("max_scores", [P, 2, 2, CH], F32))
        (q_lo, k_lo, k_hi, q_hi, ones_set, v_ready, max_ready, max_read, neg_ready, max_turned, max_copied, rows_moved,
         s_ready, exp_done, pv_done, acc_read, split_step, stored0, stored1) = make_sems(
            nc, ctx, "at", "qlo klo khi qhi ones v maxready maxread neg maxturned maxcopied rows s exp pv accread "
            "split stored0 stored1")
        stored = (stored0, stored1)
        PIECE = 16 * len(Q_SLOTS)
        LO, HI = slice(0, QH), slice(QH, S)
        turned = mx[:, 0, 0, :].bitcast(BF16)[0:NPART * NT, 0:P]

        units = ([(t, c) for t in range(NT // 2) for c in range(NC // 2)]
                 + [(t, c) for t in range(NT // 2) for c in range(NC // 2, NC)]
                 + [(t, c) for t in range(NT // 2, NT) for c in range(NC)])

        def units_until(step, quarter):
            return min(MAXU, MAXU * (4 * step + quarter) // (4 * MAX_STEPS))

        def heads(eng, body):
            body(0, 0, True, False)
            with eng.Fori(0, (H - 2) // 2) as pair:
                body(2 * pair + 1, 1, False, False)
                body(2 * pair + 2, 0, False, False)
            body(H - 1, 1, False, True)

        with nc.Block() as block:
            @block.sync
            def _(sp):
                def load(rows, which, slots, h, par, cols, sem):
                    for n, part in enumerate(slots):
                        sp.dma_start(rows[n * DK:(n + 1) * DK, par, cols],
                                     mem.qk_parts[which, part, bass.ds(h * DK, DK), cols]).then_inc(sem, 16)

                def store(h, half):
                    sp.wait_ge(acc_read, 2 * h + half + 1)
                    for j in range(4):
                        sp.dma_start(mem.att_t[bass.ds(h * DK, DK), half * QH + j * CH:half * QH + (j + 1) * CH],
                                     acc_sb[32 * j:32 * j + DK, half, :]).then_inc(stored[half], 16)
                    sp.dma_start(mem.sums[bass.ds(h * NC + half * 4, 4), :],
                                 acc_sb[DK:DK + 97:32, half, :]).then_inc(stored[half], 16)

                def move_max(h, par):
                    sp.wait_ge(max_copied, h + 1)
                    for n in range(NPART):
                        sp.dma_start(q_rows[KR + n:KR + n + 1, par, :].rearrange("o (t q) -> o t q", q=P),
                                     max_rows[n * NT:(n + 1) * NT, :]).then_inc(rows_moved, 16)

                def head(h, par, first=False, loads=True):
                    if not first:
                        store(h - 1, 1)
                    if loads:
                        sp.wait_ge(s_ready, h * (4 * STEPS) + 2 * STEPS)
                        load(q_rows, 0, Q_SLOTS, h + 2, par, LO, q_lo)
                    store(h, 0)
                    if loads:
                        sp.wait_ge(s_ready, h * (4 * STEPS) + 3 * STEPS)
                        load(k_rows, 1, K_SLOTS, h + 2, par, LO, k_lo)
                    move_max(h + 1, 1 - par)
                    if loads:
                        sp.wait_ge(s_ready, h * (4 * STEPS) + 4 * STEPS)
                        load(k_rows, 1, K_SLOTS, h + 2, par, HI, k_hi)
                        load(q_rows, 0, Q_SLOTS, h + 2, par, HI, q_hi)

                for h in range(2):
                    load(q_rows, 0, Q_SLOTS, h, h, LO, q_lo)
                    load(k_rows, 1, K_SLOTS, h, h, LO, k_lo)
                    load(k_rows, 1, K_SLOTS, h, h, HI, k_hi)
                    load(q_rows, 0, Q_SLOTS, h, h, HI, q_hi)
                    if h == 0:
                        sp.wait_ge(max_ready, MAXU // 4 + 1)
                move_max(0, 0)
                head(0, 0, first=True)
                with sp.Fori(0, (H - 4) // 2) as pair:
                    head(2 * pair + 1, 1)
                    head(2 * pair + 2, 0)
                head(H - 3, 1)
                head(H - 2, 0, loads=False)
                store(H - 2, 1)
                store(H - 1, 0)
                store(H - 1, 1)
                for s in stored:
                    sp.wait_ge(s, 16 * 5 * H)

            @block.gpsimd
            def _(pool):
                nc.gpsimd.memset(v_ones[:], 1.0).then_inc(ones_set, 1)
                pool.wait_ge(ones_set, 1)
                nc.gpsimd.memset(k_rows[KR:P, :, :], 1.0).then_inc(ones_set, 1)
                pool.wait_ge(ones_set, 2)

                def copy_v(h, par):
                    nc.gpsimd.tensor_copy(v_ones[:, par, :, 0:DK], mem.v[:, :, bass.ds(h * DK, DK)]).then_inc(v_ready, 1)

                copy_v(0, 0)
                copy_v(1, 1)
                with pool.Fori(0, (H - 2) // 2) as pair:
                    for par in range(2):
                        pool.wait_ge(pv_done, (2 * pair + par + 1) * STEPS)
                        copy_v(2 * pair + 2 + par, par)

            @block.tensor
            def _(pe):
                def max_unit(h, par, n):
                    t, c = units[n]
                    if n == 0:
                        pe.wait_ge(q_lo, (h + 1) * PIECE)
                        pe.wait_ge(k_lo, (h + 1) * PIECE)
                        if not isinstance(h, int) or h > 0:
                            pe.wait_ge(max_copied, h)
                    if (t, c) == (0, NC // 2):
                        pe.wait_ge(k_hi, (h + 1) * PIECE)
                    if (t, c) == (NT // 2, 0):
                        pe.wait_ge(q_hi, (h + 1) * PIECE)
                    pair = h * (MAXU // 2) + n // 2
                    if n % 2 == 0 and (not isinstance(pair, int) or pair >= 2):
                        pe.wait_ge(max_read, pair - 1)
                    mm = nc.tensor.matmul(mx[:, n // 2 % 2, n % 2, :], q_rows[0:KR, par, t * P:(t + 1) * P],
                                          k_rows[0:KR, par, c * CH:(c + 1) * CH], start=True, stop=True)
                    if n % 2:
                        mm.then_inc(max_ready, 1)

                def turn_max(h):
                    pe.wait_ge(neg_ready, h + 1)
                    nc.tensor.transpose(turned, neg_parts[:].rearrange("p s t -> p (s t)"),
                                        mem.ident_b[:]).then_inc(max_turned, 1)

                def scores(h, par, t, j):
                    half, kt, n = t // NKT, t % NKT, 4 * t + j
                    if n == 0:
                        pe.wait_ge(rows_moved, (h + 1) * 16 * NPART)
                    ago = 1 if n == 0 else SB
                    done = h * (4 * STEPS) + n + 1 - ago
                    if not isinstance(done, int) or done > 0:
                        pe.wait_ge(exp_done, done)
                    q0 = half * QH + j * CH
                    nc.tensor.matmul(sc[:, n % SB, :], k_rows[0:KM, par, kt * P:(kt + 1) * P],
                                     q_rows[0:KM, par, q0:q0 + CH], start=True, stop=True).then_inc(s_ready, 1)

                def head(h, par, first, last_head):
                    for t in range(STEPS):
                        half, kt = t // NKT, t % NKT
                        for j in range(4):
                            if j == 3:
                                if t == 0:
                                    pe.wait_ge(v_ready, h + 1)
                                if kt == 0 and not (first and t == 0):
                                    pe.wait_ge(acc_read, 2 * h + half)
                                pe.wait_ge(exp_done, h * (4 * STEPS) + 4 * t + 4)
                                for i in range(4):
                                    last = nc.tensor.matmul(acc[32 * i:32 * i + VW, :], v_ones[:, par, kt, :],
                                                            prob[:, t % 2, i * CH:(i + 1) * CH], start=(kt == 0),
                                                            stop=(kt == NKT - 1), tile_position=(0, 32 * i))
                                last.then_inc(pv_done, 1)
                            if t < STEPS - 1:
                                scores(h, par, t + 1, j)
                            elif not last_head:
                                scores(h + 1, 1 - par, 0, j)
                            if not last_head:
                                for n in range(units_until(t, j), units_until(t, j + 1)):
                                    max_unit(h + 1, 1 - par, n)
                        if t == MROW_STEP and not last_head:
                            turn_max(h + 1)

                pe.wait_ge(ones_set, 2)
                for n in range(MAXU):
                    max_unit(0, 0, n)
                turn_max(0)
                for j in range(4):
                    scores(0, 0, 0, j)
                heads(pe, head)

            @block.scalar
            def _(act):
                def copy_block(h, half):
                    act.wait_ge(pv_done, h * STEPS + (half + 1) * NKT)
                    if not isinstance(h, int) or h > 0:
                        act.wait_ge(stored[half], h * (16 * 5))
                    nc.scalar.activation(acc_sb[:, half, :], acc[:], ACT.Copy).then_inc(acc_read, 1)

                def head(h, par, first, last_head):
                    for t in range(STEPS):
                        if not (first and t < 2):
                            act.wait_ge(pv_done, h * STEPS + t - 1)
                        for j in range(4):
                            n = 4 * t + j
                            act.wait_ge(s_ready, h * (4 * STEPS) + n + 1)
                            nc.scalar.activation(prob[:, t % 2, j * CH:(j + 1) * CH], sc[:, n % SB, :], ACT.Exp,
                                                 scale=SCALE).then_inc(exp_done, 1)
                        if t == 0 and not first:
                            copy_block(h - 1, 1)
                        if t == NKT:
                            copy_block(h, 0)

                heads(act, head)
                copy_block(H - 1, 1)

            @block.vector
            def _(dve):
                def max_pair(h, m):
                    t, c = units[2 * m]
                    dve.wait_ge(max_ready, h * (MAXU // 2) + m + 1)
                    nc.vector.tensor_reduce(part_max[:, t, c:c + 2], mx[:, m % 2, :, :], AXX, ALU.max).then_inc(max_read, 1)

                def split_max(h):
                    dve.wait_ge(max_read, (h + 1) * (MAXU // 2))
                    steps = Chain(dve, split_step, h * 4)
                    steps.link(nc.vector.tensor_reduce(neg_max[:], part_max[:], AXX, ALU.max, negate=True))
                    steps.link(nc.vector.tensor_copy(neg_parts[:, 0, :], neg_max[:]))
                    steps.link(nc.vector.tensor_tensor(neg_rest[:], neg_max[:], neg_parts[:, 0, :], ALU.subtract))
                    steps.link(nc.vector.tensor_copy(neg_parts[:, 1, :], neg_rest[:]))
                    nc.vector.tensor_tensor(neg_parts[:, 2, :], neg_rest[:], neg_parts[:, 1, :],
                                            ALU.subtract).then_inc(neg_ready, 1)
                    if not isinstance(h, int) or h > 0:
                        dve.wait_ge(rows_moved, h * (16 * NPART))
                    dve.wait_ge(max_turned, h + 1)
                    nc.vector.tensor_copy(max_rows[:], turned).then_inc(max_copied, 1)

                def head(h, par, first, last_head):
                    if not last_head:
                        for m in range(MAXU // 2):
                            max_pair(h + 1, m)
                        split_max(h + 1)

                for m in range(MAXU // 2):
                    max_pair(0, m)
                split_max(0)
                heads(dve, head)


def attention_output(nc, mem, io):
    with ExitStack() as ctx:
        def sb(name, shape, dt):
            return ctx.enter_context(nc.sbuf_tensor(name, shape, dt))

        w_o = sb("w_o", [P, DH, D], F32)
        b_o = sb("b_o", [P, 1, D], F32)
        att = sb("att_all", [P, DH, S], F32)
        att_n = sb("att_norm", [P, 2, DH, CH], F32)
        sums = sb("sums_all", [P, CH], F32)
        recip = sb("sums_recip", [P, CH], F32)
        to_rows = sb("to_rows", [P, DH, NC, P], F32)
        bc = ctx.enter_context(nc.psum_tensor("recip_rows", [P, 2, DH, CH], F32))
        ob = ctx.enter_context(nc.psum_tensor("ao_out", [P, 2, TPC, D], F32))
        (loaded, sums_loaded, one_hot, bias_added, recip_ready, rows_ready, att_ready, o_ready, x_ready,
         dve_passed) = make_sems(
            nc, ctx, "ao", "loaded sumsloaded onehot bias recip rows att o x passed")
        att_loaded = make_sems(nc, ctx, "ao", " ".join(f"att{i}" for i in range(NC)))

        with nc.Block() as block:
            @block.sync
            def _(sp):
                sp.dma_start(sums[:], mem.sums).then_inc(sums_loaded, 16)
                for i in range(NC):
                    sp.dma_start(att[:, :, i * CH:(i + 1) * CH],
                                 mem.att_t[:, i * CH:(i + 1) * CH].rearrange("(h p) t -> p h t", p=P)).then_inc(att_loaded[i], 16)
                    if i == 0:
                        sp.dma_start(w_o[:], io.w_o.rearrange("(h p) o -> p h o", p=P)).then_inc(loaded, 16)
                        sp.dma_start(b_o[:, 0, :], io.b_o).then_inc(loaded, 16)

            @block.gpsimd
            def _(pool):
                nc.gpsimd.memset(to_rows[:], 0.0).then_inc(one_hot, 1)
                pool.wait_ge(one_hot, 1)
                v = to_rows[:].rearrange("p h c (a r) -> p h c a r", r=DK)
                nc.gpsimd.affine_select(out=v, in_=v, compare_op=ALU.not_equal, fill=1.0, base=0,
                                        pattern=[[-NC * H // DH, DH], [-1, NC], [-NC, H // DH], [0, DK]],
                                        channel_multiplier=1).then_inc(one_hot, 1)
                pool.wait_ge(loaded, 32)
                with pool.Fori(0, NC) as i:
                    xs = mem.x[:, bass.ts(i, TPC), :]
                    nc.gpsimd.tensor_tensor(xs, xs, b_o[:].to_broadcast([P, TPC, D]), ALU.add).then_inc(bias_added, 1)

            @block.tensor
            def _(pe):
                def rows(i):
                    if i >= 2:
                        pe.wait_ge(att_ready, i - 1)
                    for h in range(DH):
                        last = nc.tensor.matmul(bc[:, i % 2, h, :], to_rows[:, h, i, :], recip[:], start=True, stop=True)
                    last.then_inc(rows_ready, 1)

                pe.wait_ge(one_hot, 2)
                pe.wait_ge(recip_ready, 1)
                rows(0)
                pe.wait_ge(loaded, 32)
                for i in range(NC):
                    if i < NC - 1:
                        rows(i + 1)
                    pe.wait_ge(att_ready, i + 1)
                    if i >= 2:
                        pe.wait_ge(x_ready, i - 1)
                    for k in range(TPC):
                        for h in range(DH):
                            last = nc.tensor.matmul(ob[:, i % 2, k, :], att_n[:, i % 2, h, k * P:(k + 1) * P],
                                                    w_o[:, h, :], start=(h == 0), stop=(h == DH - 1))
                    last.then_inc(o_ready, 1)

            @block.vector
            def _(dve):
                def normalise(i):
                    dve.wait_ge(att_loaded[i], 16)
                    dve.wait_ge(rows_ready, i + 1)
                    if i >= 2:
                        dve.wait_ge(o_ready, i - 1)
                    nc.vector.tensor_tensor(att_n[:, i % 2], bc[:, i % 2], att[:, :, i * CH:(i + 1) * CH],
                                            ALU.mult).then_inc(att_ready, 1)

                dve.wait_ge(sums_loaded, 16)
                nc.vector.reciprocal(recip[:], sums[:]).then_inc(recip_ready, 1)
                normalise(0)
                for i in range(NC):
                    if i < NC - 1:
                        normalise(i + 1)
                    dve.wait_ge(bias_added, i + 1)
                    dve.wait_ge(o_ready, i + 1)
                    xs = mem.x[:, i * TPC:(i + 1) * TPC, :]
                    nc.vector.tensor_tensor(xs, ob[:, i % 2], xs, ALU.add).then_inc(x_ready, 1)
                    dve.wait_ge(x_ready, i + 1)
                    for k in range(TPC):
                        layer_stats(nc, mem, i * TPC + k)


def hybrid_kernel(nc, io, out):
    with ExitStack() as ctx:
        def sb(name, shape, dt, where=ctx):
            return where.enter_context(nc.sbuf_tensor(name, shape, dt))

        mem = Mem()
        mem.x = sb("x_res", [P, NT, D], F32)
        mem.xn = sb("xn", [P, TPC, D], F32)
        mem.six = sb("bn_six", [P, NT, 6], F32)
        mem.mv = sb("mean_var", [P, NT, 2], F32)
        mem.rstd = sb("rstd", [P, NT, 1], F32)
        mem.ident = sb("ident", [P, P], F32)
        mem.ident_b = sb("ident_b", [P, P], BF16)
        mem.eps = sb("eps", [P, 1], F32)
        mem.w_ffn = sb("w_ffn", [P, DH, 2 * D], F32)
        with ExitStack() as scan:
            mem.xp = sb("x_parts", [P, NPART, DH, S], BF16, scan)
            mem.b_rep = sb("b_rep", [P, S], F32, scan)
            mem.c_rep = sb("c_rep", [P, S], F32, scan)
            mem.delta = sb("delta", [P, S], F32, scan)
            mem.a_scale = sb("a_scale", [P, NJ], F32, scan)
            mem.spread = sb("spread", [P, NJH, P], BF16, scan)
            mem.gather = sb("gather", [P, NJ, 32], F32, scan)
            mem.carry = sb("carry", [P, NJ], F32, scan)
            norm_and_project(nc, mem, io)
            selective_scan(nc, mem)
        ffn_weights(nc, mem, io)
        ffn(nc, mem, "f1")
        mem.qk_parts = nc.dram_tensor("qk_parts", [2, NPART, D, S], BF16, kind="Internal").ap()
        attn = ExitStack()
        mem.v = sb("v_all", [P, NKT, D], F32, attn)
        attention_project(nc, mem, io)
        mem.att_t = nc.dram_tensor("att_t", [D, S], F32, kind="Internal").ap()
        mem.sums = nc.dram_tensor("att_sums", [H * NC, CH], F32, kind="Internal").ap()
        attention(nc, mem)
        attn.close()
        attention_output(nc, mem, io)
        ffn(nc, mem, "f2", out)


def rope_tables():
    freq = (1.0 / np.float32(10000.0) ** (np.arange(0, DK, 2, dtype=np.float32) / np.float32(DK))).astype(np.float32)
    ang = (np.arange(S, dtype=np.float32)[None, :] * freq[:, None]).astype(np.float32)
    cos, sin = np.cos(ang), np.sin(ang)
    return np.stack([np.tile(np.concatenate([cos, cos]), (P // DK, 1)),
                     np.tile(np.concatenate([-sin, sin]), (P // DK, 1))]).astype(np.float32)


def kernel(**inputs):
    import concourse.bacc as bacc
    from concourse.bass_utils import run_bass_kernel_spmd

    a = {n.removeprefix("L0_"): np.asarray(v) for n, v in inputs.items()}
    heads = lambda w: w.reshape(*w.shape[:-1], H, 2, DK // 2)
    swap = lambda w: heads(w)[..., ::-1, :].reshape(w.shape)
    by_state = lambda w: np.tile(w.T, (1, CPT))
    arrays = {
        "x": a["attn_a_sequence"],
        "a_tiles": a["attn_a_A"].reshape(NJ, P).T,
        "w_bcd": np.stack([by_state(a["attn_a_W_B"]), by_state(a["attn_a_W_C"]),
                           np.tile(a["attn_a_W_Delta"].T, (1, P))], axis=1),
        "bias_bcd": np.stack([np.tile(a["attn_a_b_B"], CPT), np.tile(a["attn_a_b_C"], CPT),
                              np.tile(a["attn_a_b_Delta"], P), np.tile(a["attn_a_bias_Delta"], P)], axis=1),
        "theta": a["ffn_theta"], "theta_noise": a["ffn_theta_noise"],
        "phi": a["ffn_phi"], "phi_noise": a["ffn_phi_noise"],
        "w_qk": np.stack([np.stack([w, swap(w)]) for w in (a["attn_b_Wq"], a["attn_b_Wk"])]),
        "b_qk": np.stack([np.stack([b, swap(b)]) for b in (a["attn_b_bq"], a["attn_b_bk"])])
        .reshape(2, 2, DH, P).transpose(3, 0, 1, 2),
        "w_v": a["attn_b_Wv"], "b_v": np.tile(a["attn_b_bv"], (P, 1)),
        "w_o": a["attn_b_Wo"], "b_o": np.tile(a["attn_b_bo"], (P, 1)),
        "trig": rope_tables(),
    }
    nc = bacc.Bacc("TRN2", target_bir_lowering=False, num_devices=1)
    io = Mem()
    arrays = {f"in_{name}": np.ascontiguousarray(value) for name, value in arrays.items()}
    for name, value in arrays.items():
        io.__dict__[name.removeprefix("in_")] = nc.dram_tensor(name, value.shape, F32, kind="ExternalInput").ap()
    out = nc.dram_tensor("out", (1, S, D), F32, kind="ExternalOutput").ap()
    hybrid_kernel(nc, io, out)
    r = run_bass_kernel_spmd(nc, [arrays], core_ids=[0])
    return r.results[0]["out"]
```

```python
from contextlib import ExitStack

import numpy as np

import concourse.bass as bass
from concourse import mybir

F32 = mybir.dt.float32
BF16 = mybir.dt.bfloat16
ACT = mybir.ActivationFunctionType
ALU = mybir.AluOpType
AXX = mybir.AxisListType.X

P = 128
S = 4096
D = 256
DH = D // P
NT = S // P
TPC = 4
CH = TPC * P
NC = S // CH
NS = 16
CPT = P // NS
NJ = D // CPT
NJH = NJ // DH
SC = 1024
NSC = S // SC
TPS = SC // P
H = 16
DK = D // H
EPS = 1e-5
NPART = 3
Q_SLOTS = (0, 0, 0, 1, 1, 2)
K_SLOTS = (0, 1, 2, 0, 1, 0)
KR = DK * len(Q_SLOTS)
KM = KR + NPART
SCALE = 0.25
QH = S // 2
NKT = S // P
STEPS = 2 * NKT
SB = 3
VW = 32
PBUF = 4
QT = QH // P
MAXU = QT * NC
MAXP = MAXU // 2
LEAD = 20
TURN_AT = 3
SLOTS = MAXP + 1
TWO_PI = 2 * np.pi
C1, C2 = 6.28125, float(np.float32(TWO_PI - 6.28125))
C3 = TWO_PI - C1 - C2
ROUND = 1.5 * 2 ** 23
PI_IN = 3.1415925


class Chain:

    def __init__(self, eng, done, base=0):
        self.eng, self.done, self.base, self.n = eng, done, base, 0

    def link(self, ins):
        ins.then_inc(self.done, 1)
        self.n += 1
        self.eng.wait_ge(self.done, self.base + self.n)


class Mem:
    pass


def make_sems(nc, ctx, stage, names):
    return [ctx.enter_context(nc.semaphore(f"{stage}_{n}")) for n in names.split()]


def later(n):
    return not isinstance(n, int) or n > 0


def ends_apart(eng, n, body):
    body(0, True, False)
    with eng.Fori(1, n - 1) as i:
        body(i, False, False)
    body(n - 1, False, True)


def wait_apart(eng, sem, value, passed):
    eng.wait_ge(sem, value)
    eng.sem_inc(passed, 1)


def layer_stats(nc, mem, tile):
    return nc.vector.bn_stats(mem.six[:, tile, :], mem.x[:, tile, :])


def aggregate_stats(nc, mem, done):
    for t in range(NT):
        last = nc.vector.bn_aggr(mem.mv[:, t, :], mem.six[:, t, :])
    last.then_inc(done, 1)


def norm_and_project(nc, mem, io):
    with ExitStack() as ctx:
        def sb(name, shape, dt):
            return ctx.enter_context(nc.sbuf_tensor(name, shape, dt))

        NQ = NC // 2
        QTK = S // NQ
        w_bcd = sb("w_bcd", [P, DH, 3, P], F32)
        bias = sb("bias_bcd", [P, 4], F32)
        recip_a = sb("recip_a", [P, NJ], F32)
        mask = sb("channel_mask", [P, CPT], F32)
        xn = sb("np_xn", [P, 2, TPC, D], F32)
        xnt = sb("np_xnt", [P, 2, DH, CH], F32)
        rest = sb("np_rest", [P, 2, DH, CH], F32)
        soft = sb("np_soft", [P, QTK], F32)
        TPQ = QTK // P
        six = sb("np_six", [P, TPQ, 6], F32)
        mv = sb("np_mean_var", [P, TPQ, 2], F32)
        std = sb("np_std", [P, TPQ, 1], F32)
        rstd = sb("np_rstd", [P, TPQ, 1], F32)
        noise = sb("angle_noise", [P, DH, 2, D], F32)
        turns = sb("angle_turns", [P, DH, 2, D], F32)
        ang = mem.w_ffn[:].rearrange("p h (a o) -> p h a o", a=2)
        tp = ctx.enter_context(nc.psum_tensor("np_tp", [P, DH, CH], F32))
        pb = ctx.enter_context(nc.psum_tensor("np_proj", [P, 2, 3, CH], F32))
        (loaded, x_here, consts, pool_step, dve_step, stats_step, stats_done, std_ready, rstd_ready, xn_ready, t_ready,
         xnt_ready, hi_ready, rest_ready, mid_ready, lo_ready, proj_ready, proj_read, neg_ready, exp_ready, ln_ready,
         bias_ready, soft_added, passed, angles_loaded, angle_step) = make_sems(
            nc, ctx, "np", "loaded xhere consts poolstep dvestep statsstep stats std rstd xn t xnt hi rest mid lo proj "
            "projread neg exp ln bias softadded passed anglesloaded anglestep")
        x_loaded = make_sems(nc, ctx, "np", "x0 x1 x2 x3")

        with nc.Block() as block:
            @block.sync
            def _(sp):
                xv = io.x.rearrange("a (t p) d -> (a p) t d", p=P)
                for q in range(NQ):
                    sp.dma_start(mem.x[:, 8 * q:8 * q + 8, :], xv[:, 8 * q:8 * q + 8, :]).then_inc(x_loaded[q], 16)
                    if q == 0:
                        sp.dma_start(w_bcd[:], io.w_bcd.rearrange("(h p) j c -> p h j c", p=P)).then_inc(loaded, 16)
                        sp.dma_start(bias[:], io.bias_bcd).then_inc(loaded, 16)
                        sp.dma_start(mem.a_scale[:], io.a_tiles).then_inc(loaded, 16)
                for n, (w, e) in enumerate(((io.theta, io.theta_noise), (io.phi, io.phi_noise))):
                    sp.dma_start(ang[:, :, n, :], w.rearrange("(h p) o -> p h o", p=P)).then_inc(angles_loaded, 16)
                    sp.dma_start(noise[:, :, n, :], e.rearrange("(h p) o -> p h o", p=P)).then_inc(angles_loaded, 16)
                for q in range(NQ):
                    sp.wait_ge(x_loaded[q], 16)
                    sp.sem_inc(x_here, 1)

            @block.gpsimd
            def _(pool):
                steps = Chain(pool, pool_step)
                steps.link(nc.gpsimd.memset(mem.eps[:], EPS))
                steps.link(nc.gpsimd.memset(mem.ident[:], 0.0))
                steps.link(nc.gpsimd.affine_select(
                    out=mem.ident[:], in_=mem.ident[:], compare_op=ALU.not_equal, fill=1.0, base=0,
                    pattern=[[-1, P]], channel_multiplier=1))
                pool.sem_inc(consts, 1)
                steps.link(nc.gpsimd.memset(mask[:], 1.0))
                steps.link(nc.gpsimd.affine_select(out=mask[:], in_=mask[:], compare_op=ALU.is_ge, fill=0.0, base=0,
                                                   pattern=[[-NS, CPT]], channel_multiplier=1))
                steps.link(nc.gpsimd.affine_select(out=mask[:], in_=mask[:], compare_op=ALU.is_ge, fill=0.0,
                                                   base=NS - 1, pattern=[[NS, CPT]], channel_multiplier=-1))
                steps.link(nc.gpsimd.memset(mem.gather[:], 0.0))
                pool.sem_inc(consts, 1)

                def what_hi_leaves(i, b):
                    pool.wait_ge(hi_ready, i + 1)
                    if later(i - 1):
                        pool.wait_ge(lo_ready, i - 1)
                    nc.gpsimd.tensor_tensor(rest[:, b], xnt[:, b], mem.xp[:, 0, :, bass.ts(i, CH)],
                                            ALU.subtract).then_inc(rest_ready, 1)

                def quarter(p, first, last_quarter):
                    for b in range(2):
                        what_hi_leaves(2 * p + b, b)
                    if first:
                        steps.link(nc.gpsimd.tensor_copy(mem.ident_b[:], mem.ident[:]))
                        steps.link(nc.gpsimd.memset(mem.spread[:], 0.0))
                        v = mem.spread[:].rearrange("p j (a n) -> p j a n", n=NS)
                        steps.link(nc.gpsimd.affine_select(
                            out=v, in_=v, compare_op=ALU.not_equal, fill=1.0, base=0,
                            pattern=[[-CPT, NJH], [-1, CPT], [0, NS]], channel_multiplier=1))
                        steps.link(nc.gpsimd.memset(mem.carry[:], 0.0))

                ends_apart(pool, NQ, quarter)

            @block.vector
            def _(dve):
                def quarter_stats(q):
                    dve.wait_ge(x_here, q + 1)
                    if later(q):
                        dve.wait_ge(stats_done, q)
                    for k in range(TPQ):
                        last = nc.vector.bn_stats(six[:, k, :], mem.x[:, TPQ * q + k, :])
                    last.then_inc(stats_step, 1)
                    wait_apart(dve, stats_step, q + 1, passed)
                    if later(q):
                        wait_apart(dve, xn_ready, 2 * q, passed)
                    for k in range(TPQ):
                        last = nc.vector.bn_aggr(mv[:, k, :], six[:, k, :])
                    last.then_inc(stats_done, 1)

                def reciprocals(q):
                    dve.wait_ge(std_ready, q + 1)
                    nc.vector.reciprocal(rstd[:], std[:]).then_inc(rstd_ready, 1)
                    wait_apart(dve, rstd_ready, q + 1, passed)

                def normalise(i, b):
                    if later(i - 1):
                        dve.wait_ge(t_ready, i - 1)
                    for k in range(TPC):
                        n = b * TPC + k
                        last = nc.vector.tensor_scalar(xn[:, b, k, :], mem.x[:, i * TPC + k, :], mv[:, n, 0:1],
                                                       rstd[:, n, 0:1], ALU.subtract, ALU.mult)
                    last.then_inc(xn_ready, 1)

                def low(i, b):
                    dve.wait_ge(mid_ready, i + 1)
                    nc.vector.tensor_tensor(mem.xp[:, 2, :, bass.ts(i, CH)], rest[:, b],
                                            mem.xp[:, 1, :, bass.ts(i, CH)], ALU.subtract).then_inc(lo_ready, 1)

                def minus_abs(q):
                    dve.wait_ge(proj_read, 2 * q + 2)
                    if later(q):
                        dve.wait_ge(soft_added, q)
                    z = mem.delta[:, bass.ts(q, QTK)]
                    nc.vector.scalar_tensor_tensor(soft[:], z, -1.0, z, ALU.mult, ALU.min).then_inc(neg_ready, 1)

                def softplus(q):
                    dve.wait_ge(ln_ready, q + 1)
                    z = mem.delta[:, bass.ts(q, QTK)]
                    nc.vector.scalar_tensor_tensor(z, z, 0.0, soft[:], ALU.max, ALU.add).then_inc(soft_added, 1)

                steps = Chain(dve, angle_step)

                def angles():
                    dve.wait_ge(angles_loaded, 64)
                    steps.link(nc.vector.tensor_tensor(ang, ang, noise[:], ALU.add))
                    steps.link(nc.vector.tensor_scalar(turns[:], ang, 1 / TWO_PI, None, ALU.mult))
                    steps.link(nc.vector.tensor_scalar(turns[:, :, 0, :], turns[:, :, 0, :], 0.25, None, ALU.add))
                    steps.link(nc.vector.tensor_scalar(turns[:], turns[:], ROUND, None, ALU.add))
                    steps.link(nc.vector.tensor_scalar(turns[:], turns[:], -ROUND, None, ALU.add))

                def in_range():
                    for c in (C1, C2, C3):
                        steps.link(nc.vector.scalar_tensor_tensor(ang, turns[:], -c, ang, ALU.mult, ALU.add))
                    steps.link(nc.vector.tensor_scalar(ang[:, :, 0, :], ang[:, :, 0, :], np.pi / 2, None, ALU.add))
                    steps.link(nc.vector.tensor_scalar(ang, ang, PI_IN, -PI_IN, ALU.min, ALU.max))

                def quarter(p, first, last_quarter):
                    if not last_quarter:
                        quarter_stats(p + 1)
                    if not first:
                        low(2 * p - 1, 1)
                    if not last_quarter:
                        reciprocals(p + 1)
                        normalise(2 * p + 2, 0)
                    if not first:
                        minus_abs(p - 1)
                    if last_quarter:
                        angles()
                    low(2 * p, 0)
                    if not last_quarter:
                        normalise(2 * p + 3, 1)
                    if not first:
                        softplus(p - 1)

                quarter_stats(0)
                reciprocals(0)
                normalise(0, 0)
                normalise(1, 1)
                gather_steps = Chain(dve, dve_step)
                dve.wait_ge(loaded, 48)
                nc.vector.tensor_tensor(bias[:, 2:3], bias[:, 2:3], bias[:, 3:4], ALU.add).then_inc(bias_ready, 1)
                dve.wait_ge(consts, 2)
                gather_steps.link(nc.vector.reciprocal(recip_a[:], mem.a_scale[:]))
                g = mem.gather[:].rearrange("p (g r) c -> p g r c", r=4)
                ra = recip_a[:].rearrange("p (g r) -> p g r", r=4)
                for r in range(4):
                    gather_steps.link(nc.vector.tensor_tensor(
                        g[:, :, r, CPT * r:CPT * r + CPT], mask[:].unsqueeze(1).to_broadcast([P, NJ // 4, CPT]),
                        ra[:, :, r].unsqueeze(2).to_broadcast([P, NJ // 4, CPT]), ALU.mult))
                ends_apart(dve, NQ, quarter)
                minus_abs(NQ - 1)
                low(NC - 1, 1)
                in_range()
                softplus(NQ - 1)

            @block.scalar
            def _(act):
                def deviations(q):
                    act.wait_ge(stats_done, q + 1)
                    nc.scalar.activation(std[:], mv[:, :, 1:2], ACT.Sqrt, bias=mem.eps[:, 0:1]).then_inc(std_ready, 1)

                def copy_turned(i, b):
                    act.wait_ge(t_ready, i + 1)
                    if later(i - 1):
                        act.wait_ge(proj_ready, i - 1)
                        act.wait_ge(rest_ready, i - 1)
                    nc.scalar.activation(xnt[:, b], tp[:], ACT.Copy).then_inc(xnt_ready, 1)

                def high(i, b):
                    act.wait_ge(xnt_ready, i + 1)
                    nc.scalar.activation(mem.xp[:, 0, :, bass.ts(i, CH)], xnt[:, b], ACT.Copy).then_inc(hi_ready, 1)

                def middle(i, b):
                    act.wait_ge(rest_ready, i + 1)
                    nc.scalar.activation(mem.xp[:, 1, :, bass.ts(i, CH)], rest[:, b], ACT.Copy).then_inc(mid_ready, 1)

                def outputs(i, b):
                    act.wait_ge(proj_ready, i + 1)
                    for n, dst in enumerate((mem.b_rep, mem.c_rep, mem.delta)):
                        last = nc.scalar.activation(dst[:, bass.ts(i, CH)], pb[:, b, n, :], ACT.Identity,
                                                    bias=bias[:, n:n + 1])
                    last.then_inc(proj_read, 1)

                def log_exp(q):
                    act.wait_ge(neg_ready, q + 1)
                    nc.scalar.activation(soft[:], soft[:], ACT.Exp).then_inc(exp_ready, 1)
                    act.wait_ge(exp_ready, q + 1)
                    nc.scalar.activation(soft[:], soft[:], ACT.Ln, bias=1.0).then_inc(ln_ready, 1)

                def quarter(p, first, last_quarter):
                    for b in range(2):
                        i = 2 * p + b
                        if not (last_quarter and b == 1):
                            copy_turned(i + 1, 1 - b)
                        high(i, b)
                        if not (first and b == 0):
                            middle(i - 1, 1 - b)
                        if b == 0 and not last_quarter:
                            deviations(p + 1)
                        if not (first and b == 0):
                            outputs(i - 1, 1 - b)
                        if b == 1 and not first:
                            log_exp(p - 1)

                act.wait_ge(consts, 1)
                deviations(0)
                copy_turned(0, 0)
                act.wait_ge(bias_ready, 1)
                ends_apart(act, NQ, quarter)
                middle(NC - 1, 1)
                outputs(NC - 1, 1)
                log_exp(NQ - 1)

            @block.tensor
            def _(pe):
                def turn(i, b):
                    pe.wait_ge(xn_ready, i + 1)
                    for h in range(DH):
                        for k in range(TPC):
                            last = nc.tensor.transpose(tp[:, h, k * P:(k + 1) * P], xn[:, b, k, h * P:(h + 1) * P],
                                                       mem.ident[:])
                    last.then_inc(t_ready, 1)

                def quarter(p, first, last_quarter):
                    for b in range(2):
                        i = 2 * p + b
                        pe.wait_ge(xnt_ready, i + 1)
                        if not (last_quarter and b == 1):
                            turn(i + 1, 1 - b)
                        if later(i - 1):
                            pe.wait_ge(proj_read, i - 1)
                        for n in range(3):
                            for h in range(DH):
                                last = nc.tensor.matmul(pb[:, b, n, :], w_bcd[:, h, n, :], xnt[:, b, h, :],
                                                        start=(h == 0), stop=(h == DH - 1))
                        last.then_inc(proj_ready, 1)

                pe.wait_ge(consts, 1)
                pe.wait_ge(loaded, 48)
                turn(0, 0)
                ends_apart(pe, NQ, quarter)


def selective_scan(nc, mem):
    with ExitStack() as ctx:
        def sb(name, shape, dt):
            return ctx.enter_context(nc.sbuf_tensor(name, shape, dt))

        decay = sb("decay", [P, 2, SC], F32)
        w = sb("scan_w", [P, 2, SC], F32)
        u = sb("scan_u", [P, 2, SC], F32)
        st = sb("scan_state", [P, 2, SC], F32)
        hc = sb("scan_hc", [P, 2, SC], F32)
        ysb = sb("scan_y", [P, SC], F32)
        xr = ctx.enter_context(nc.psum_tensor("x_spread", [P, 2, SC], F32))
        yb = ctx.enter_context(nc.psum_tensor("y_sum", [P, SC], F32))
        ty = ctx.enter_context(nc.psum_tensor("y_tokens", [P, TPS, P], F32))
        (xr_ready, w_done, decay_ready, u_done, scan_done, carry_saved, hc_done, y_done, y_copied, y_turned,
         x_added, act_passed, pool_passed) = make_sems(
            nc, ctx, "ss", "xr w decay u scan carry hc y ycopied yturned xadded actpassed poolpassed")

        with nc.Block() as block:
            @block.tensor
            def _(pe):
                def spread_x(c, j, n):
                    pe.wait_ge(w_done, n + 1)
                    for b in range(SC // CH):
                        for part in range(NPART):
                            last = nc.tensor.matmul(
                                xr[:, j % 2, b * CH:(b + 1) * CH], mem.spread[:, j % NJH, :],
                                mem.xp[:, part, j // NJH, bass.ds(c * SC + b * CH, CH)],
                                start=(part == 0), stop=(part == NPART - 1))
                    last.then_inc(xr_ready, 1)

                def turn_y(k):
                    pe.wait_ge(y_copied, k)
                    pe.wait_ge(x_added, k)
                    for t in range(TPS):
                        last = nc.tensor.transpose(ty[:, t, :], ysb[:, t * P:(t + 1) * P], mem.ident[:])
                    last.then_inc(y_turned, 1)

                def chunk(c, first, last_chunk):
                    for j in range(NJ):
                        n, k, jj = c * NJ + j, c * DH + j // NJH, j % NJH
                        if j < NJ - 3:
                            spread_x(c, j + 3, n + 3)
                        elif not last_chunk:
                            spread_x(c + 1, j + 3 - NJ, n + 3)
                        pe.wait_ge(hc_done, n + 3)
                        if jj == 0 and not (first and j == 0):
                            pe.wait_ge(y_copied, k)
                        g, r = jj // 4, jj % 4
                        for b in range(SC // CH):
                            last = nc.tensor.matmul(
                                yb[32 * g:32 * g + 32, b * CH:(b + 1) * CH], mem.gather[:, j, :],
                                hc[:, j % 2, b * CH:(b + 1) * CH], start=(r == 0), stop=(r == 3),
                                tile_position=(0, 32 * g))
                        last.then_inc(y_done, 1)
                        if jj == 2 and not (first and j < NJH):
                            turn_y(k)

                spread_x(0, 0, 0)
                spread_x(0, 1, 1)
                spread_x(0, 2, 2)
                ends_apart(pe, NSC, chunk)
                turn_y(NSC * DH)

            @block.scalar
            def _(act):
                act.sem_inc(scan_done, 2)
                act.sem_inc(y_turned, 1)

                def copy_y(k):
                    act.wait_ge(y_done, k * NJH + 2)
                    act.wait_ge(y_turned, k)
                    nc.scalar.activation(ysb[:], yb[:], ACT.Copy).then_inc(y_copied, 1)

                def chunk(c, first, last_chunk):
                    for j in range(NJ):
                        wait_apart(act, scan_done, c * NJ + j + 1, act_passed)
                        nc.scalar.activation(decay[:, j % 2, :], mem.delta[:, bass.ts(c, SC)], ACT.Exp,
                                             scale=mem.a_scale[:, j:j + 1]).then_inc(decay_ready, 1)
                        if j % NJH == 2 and not (first and j < NJH):
                            copy_y(c * DH + j // NJH)
                        if first and j == 6:
                            nc.scalar.activation(mem.w_ffn[:], mem.w_ffn[:], ACT.Sin)

                ends_apart(act, NSC, chunk)
                copy_y(NSC * DH)

            @block.vector
            def _(dve):
                dve.sem_inc(w_done, 2)
                dve.sem_inc(x_added, 1)

                def add_y(k, tile, half):
                    dve.wait_ge(y_turned, k + 1)
                    xs = mem.x[:, bass.ds(tile, TPS), half * P:(half + 1) * P]
                    nc.vector.tensor_tensor(xs, ty[:], xs, ALU.add).then_inc(x_added, 1)

                def times_b(c, j, n):
                    dve.wait_ge(xr_ready, n + 1)
                    nc.vector.tensor_tensor(w[:, j % 2, :], xr[:, j % 2, :], mem.b_rep[:, bass.ts(c, SC)],
                                            ALU.mult).then_inc(w_done, 1)

                def chunk(c, first, last_chunk):
                    for j in range(NJ):
                        n, b = c * NJ + j, j % 2
                        dve.wait_ge(w_done, n + 3)
                        dve.wait_ge(decay_ready, n + 1)
                        nc.vector.scalar_tensor_tensor(u[:, b, :], decay[:, b, :], -1.0, w[:, b, :], ALU.add,
                                                       ALU.mult).then_inc(u_done, 1)
                        if j < NJ - 1:
                            times_b(c, j + 1, n + 1)
                        elif not last_chunk:
                            times_b(c + 1, 0, n + 1)
                        dve.wait_ge(u_done, n + 1)
                        dve.wait_ge(hc_done, n + 1)
                        dve.wait_ge(carry_saved, n + NJ - 1)
                        nc.vector.tensor_tensor_scan(st[:, b, :], decay[:, b, :], u[:, b, :], mem.carry[:, j:j + 1],
                                                     ALU.mult, ALU.add).then_inc(scan_done, 1)
                        if j % NJH == 4 and not (first and j < NJH):
                            add_y(c * DH + j // NJH, (c - 1) * TPS if j < NJH else c * TPS, 1 if j < NJH else 0)

                times_b(0, 0, 0)
                ends_apart(dve, NSC, chunk)
                add_y(NSC * DH, (NSC - 1) * TPS, 1)

            @block.gpsimd
            def _(pool):
                pool.sem_inc(carry_saved, NJ)
                pool.sem_inc(hc_done, 2)
                pool.sem_inc(y_done, 2)

                def chunk(c, first, last_chunk):
                    for j in range(NJ):
                        n, b = c * NJ + j, j % 2
                        wait_apart(pool, scan_done, n + 3, pool_passed)
                        nc.gpsimd.tensor_copy(mem.carry[:, j:j + 1], st[:, b, SC - 1:SC]).then_inc(carry_saved, 1)
                        wait_apart(pool, y_done, n + 1, pool_passed)
                        nc.gpsimd.tensor_tensor(hc[:, b, :], st[:, b, :], mem.c_rep[:, bass.ts(c, SC)],
                                                ALU.mult).then_inc(hc_done, 1)

                ends_apart(pool, NSC, chunk)


def ffn(nc, mem, stage, out=None):
    with ExitStack() as ctx:
        def sb(name, shape):
            return ctx.enter_context(nc.sbuf_tensor(f"{stage}_{name}", shape, F32))

        UT = 2
        NU = NT // UT
        xn = sb("xn", [P, 2, UT, D])
        xnt = sb("xnt", [P, 2, DH, UT * P])
        sq = sb("sq", [P, 2, UT, 2, D])
        amp = sb("amp", [P, 2, UT, D])
        six = sb("six", [P, 2, UT, 6])
        mv = sb("mean_var", [P, 2, UT, 2])
        std = sb("std", [P, 2, UT, 1])
        rstd = sb("rstd", [P, 2, UT, 1])
        tp = ctx.enter_context(nc.psum_tensor(f"{stage}_tp", [P, 2, DH, UT * P], F32))
        ri = ctx.enter_context(nc.psum_tensor(f"{stage}_ri", [P, 2, UT, 2, D], F32))
        (std_ready, rstd_ready, xn_ready, t_ready, xnt_ready, ri_ready, sq_ready, sum_ready, amp_ready, x_ready,
         stats_done, sums_done, stored, dve_passed) = make_sems(
            nc, ctx, stage, "std rstd xn t xnt ri sq sum amp x stats sums stored passed")

        with nc.Block() as block:
            @block.scalar
            def _(act):
                def deviations(u, b):
                    act.wait_ge(stats_done, u + 1)
                    nc.scalar.activation(std[:, b], mv[:, b, :, 1:2], ACT.Sqrt, bias=mem.eps[:, 0:1]).then_inc(std_ready, 1)

                def copy_turned(u, b):
                    act.wait_ge(t_ready, u + 1)
                    if later(u - 1):
                        act.wait_ge(ri_ready, u - 1)
                    nc.scalar.activation(xnt[:, b], tp[:, b], ACT.Copy).then_inc(xnt_ready, 1)

                def roots(u, b):
                    act.wait_ge(sum_ready, u + 1)
                    if later(u - 1):
                        act.wait_ge(x_ready, u - 1)
                    nc.scalar.activation(amp[:, b], sq[:, b, :, 0, :], ACT.Sqrt).then_inc(amp_ready, 1)

                def pair(i, first, last_pair):
                    for b in range(2):
                        u = 2 * i + b
                        if not (first and b == 0):
                            roots(u - 1, 1 - b)
                        if not last_pair:
                            deviations(u + 2, b)
                        if not (last_pair and b == 1):
                            copy_turned(u + 1, 1 - b)
                        act.wait_ge(ri_ready, u + 1)
                        if later(u - 1):
                            act.wait_ge(amp_ready, u - 1)
                        nc.scalar.activation(sq[:, b], ri[:, b], ACT.Square).then_inc(sq_ready, 1)

                deviations(0, 0)
                deviations(1, 1)
                copy_turned(0, 0)
                ends_apart(act, NU // 2, pair)
                roots(NU - 1, 1)

            @block.vector
            def _(dve):
                def unit_stats(u, b):
                    if later(u - 1):
                        dve.wait_ge(stats_done, u - 1)
                    for k in range(UT):
                        last = nc.vector.bn_stats(six[:, b, k, :], mem.x[:, u * UT + k, :])
                    last.then_inc(sums_done, 1)
                    wait_apart(dve, sums_done, u + 1, dve_passed)
                    if later(u - 1):
                        wait_apart(dve, xn_ready, u - 1, dve_passed)
                    for k in range(UT):
                        last = nc.vector.bn_aggr(mv[:, b, k, :], six[:, b, k, :])
                    last.then_inc(stats_done, 1)

                def normalise(u, b):
                    dve.wait_ge(std_ready, u + 1)
                    nc.vector.reciprocal(rstd[:, b], std[:, b]).then_inc(rstd_ready, 1)
                    wait_apart(dve, rstd_ready, u + 1, dve_passed)
                    if later(u - 1):
                        dve.wait_ge(t_ready, u - 1)
                    for k in range(UT):
                        t = u * UT + k
                        last = nc.vector.tensor_scalar(xn[:, b, k, :], mem.x[:, t, :], mv[:, b, k, 0:1],
                                                       rstd[:, b, k, :], ALU.subtract, ALU.mult)
                    last.then_inc(xn_ready, 1)

                def add_amp(u, b):
                    dve.wait_ge(amp_ready, u + 1)
                    xs = mem.x[:, bass.ts(u, UT), :]
                    nc.vector.tensor_tensor(xs, xs, amp[:, b], ALU.add).then_inc(x_ready, 1)

                def stats(u):
                    if out is None:
                        wait_apart(dve, x_ready, u + 1, dve_passed)
                        for k in range(UT):
                            layer_stats(nc, mem, u * UT + k)

                def pair(i, first, last_pair):
                    for b in range(2):
                        u = 2 * i + b
                        if not last_pair:
                            unit_stats(u + 2, b)
                        if not (first and b == 0):
                            add_amp(u - 1, 1 - b)
                        if not last_pair:
                            normalise(u + 2, b)
                        dve.wait_ge(sq_ready, u + 1)
                        nc.vector.tensor_tensor(sq[:, b, :, 0, :], sq[:, b, :, 0, :], sq[:, b, :, 1, :],
                                                ALU.add).then_inc(sum_ready, 1)
                        if not (first and b == 0):
                            stats(u - 1)

                unit_stats(0, 0)
                unit_stats(1, 1)
                normalise(0, 0)
                normalise(1, 1)
                ends_apart(dve, NU // 2, pair)
                add_amp(NU - 1, 1)
                stats(NU - 1)

            @block.tensor
            def _(pe):
                def turn(u, b):
                    pe.wait_ge(xn_ready, u + 1)
                    if later(u - 1):
                        pe.wait_ge(xnt_ready, u - 1)
                    for h in range(DH):
                        for k in range(UT):
                            last = nc.tensor.transpose(tp[:, b, h, k * P:(k + 1) * P], xn[:, b, k, h * P:(h + 1) * P],
                                                       mem.ident[:])
                    last.then_inc(t_ready, 1)

                def pair(i, first, last_pair):
                    for b in range(2):
                        u = 2 * i + b
                        pe.wait_ge(xnt_ready, u + 1)
                        if later(u - 1):
                            pe.wait_ge(sq_ready, u - 1)
                        for k in range(UT):
                            if k == UT - 1 and not (last_pair and b == 1):
                                turn(u + 1, 1 - b)
                            for h in range(DH):
                                last = nc.tensor.matmul(ri[:, b, k, :, :], xnt[:, b, h, k * P:(k + 1) * P],
                                                        mem.w_ffn[:, h, :], start=(h == 0), stop=(h == DH - 1))
                        last.then_inc(ri_ready, 1)

                turn(0, 0)
                ends_apart(pe, NU // 2, pair)

            if out is not None:
                @block.sync
                def _(sp):
                    ov = out.rearrange("a (t p) d -> (a p) t d", p=P)
                    with sp.Fori(0, NC) as i:
                        sp.wait_ge(x_ready, 2 * i + 2)
                        sp.dma_start(ov[:, bass.ts(i, TPC), :], mem.x[:, bass.ts(i, TPC), :]).then_inc(stored, 16)
                    sp.wait_ge(stored, 16 * NC)


def attention_project(nc, mem, io):
    with ExitStack() as ctx:
        def sb(name, shape, dt):
            return ctx.enter_context(nc.sbuf_tensor(name, shape, dt))

        NU = 2 * DH
        HP = P // 2
        w_qk = sb("w_qk", [P, 2, DH, D], F32)
        b_qk = sb("b_qk", [P, 2, 2, DH], F32)
        w_v = sb("w_v", [P, DH, D], F32)
        b_v = sb("b_v", [P, D], F32)
        trig = sb("rope_trig", [P, 2, S], F32)
        xn = sb("ap_xn", [P, 2, TPC, D], F32)
        xnt = sb("ap_xnt", [P, 2, DH, CH], F32)
        std = sb("ap_std", [P, NT, 1], F32)
        swapped = sb("swapped", [P, NU, CH], F32)
        term = sb("rope_terms", [P, NU, 2, CH], F32)
        roped = sb("roped", [P, NU, CH], F32)
        rest = sb("roped_rest", [P, NU, CH], F32)
        parts = sb("roped_parts", [P, NU, NPART, CH], BF16)
        tp = ctx.enter_context(nc.psum_tensor("ap_tp", [P, DH, CH], F32))
        vb = ctx.enter_context(nc.psum_tensor("ap_v", [P, TPC, D], F32))
        qb = ctx.enter_context(nc.psum_tensor("ap_qk", [P, NU, CH], F32))
        trig_loaded = make_sems(nc, ctx, "ap", "trig0 trig1 trig2 trig3")
        (loaded, trig_here, std_ready, rstd_ready, xn_ready, t_ready, xnt_ready, v_ready, v_read, qk_ready,
         swap_ready, terms, roped_ready, hi_ready, rest_ready, mid_ready, lo_ready, stats_done) = make_sems(
            nc, ctx, "ap", "loaded trighere std rstd xn t xnt v vread qk swap terms roped hi rest mid lo stats")
        stored = make_sems(nc, ctx, "ap", "stored0 stored1 stored2 stored3")

        with nc.Block() as block:
            @block.sync
            def _(sp):
                sp.dma_start(w_v[:], io.w_v.rearrange("(h p) o -> p h o", p=P)).then_inc(loaded, 16)
                sp.dma_start(b_v[:], io.b_v).then_inc(loaded, 16)
                for a in range(2):
                    sp.dma_start(w_qk[:, a], io.w_qk[a].rearrange("(h p) o -> p h o", p=P)).then_inc(loaded, 16)
                sp.dma_start(b_qk[:], io.b_qk).then_inc(loaded, 16)
                TQ = S // len(trig_loaded)
                for q, sem in enumerate(trig_loaded):
                    sp.dma_start(trig[:, :, q * TQ:(q + 1) * TQ],
                                 io.trig[:, :, q * TQ:(q + 1) * TQ].rearrange("r p t -> p r t")).then_inc(sem, 16)
                for sem in trig_loaded:
                    sp.wait_ge(sem, 16)
                    sp.sem_inc(trig_here, 1)
                with sp.Fori(0, NC) as i:
                    for n in range(NU):
                        a, h = n // DH, n % DH
                        sp.wait_ge(lo_ready, i * NU + n + 1)
                        for s in range(2):
                            sp.dma_start(
                                mem.qk_parts[a, :, s, h * HP:(h + 1) * HP, bass.ts(i, CH)].rearrange("s p t -> p s t"),
                                parts[s * HP:(s + 1) * HP, n]).then_inc(stored[n], 16)
                for s in stored:
                    sp.wait_ge(s, 32 * NC)

            @block.scalar
            def _(act):
                act.wait_ge(stats_done, 1)
                nc.scalar.activation(std[:], mem.mv[:, :, 1:2], ACT.Sqrt, bias=mem.eps[:, 0:1]).then_inc(std_ready, 1)

                def copy_turned(i, b):
                    act.wait_ge(t_ready, i + 1)
                    if later(i - 1):
                        act.wait_ge(qk_ready, (i - 1) * NU)
                    nc.scalar.activation(xnt[:, b], tp[:], ACT.Copy).then_inc(xnt_ready, 1)

                def high(g, n):
                    act.wait_ge(roped_ready, g + 1)
                    if later(g - NU + 1):
                        act.wait_ge(stored[n], (g - n) * (32 // NU))
                    nc.scalar.activation(parts[:, n, 0], roped[:, n], ACT.Copy).then_inc(hi_ready, 1)

                def middle(g, n):
                    act.wait_ge(rest_ready, g + 1)
                    nc.scalar.activation(parts[:, n, 1], rest[:, n], ACT.Copy).then_inc(mid_ready, 1)

                def pair(p, first, last_pair):
                    for b in range(2):
                        i = 2 * p + b
                        for n in range(NU):
                            g = i * NU + n
                            if n == 1 and not (last_pair and b == 1):
                                copy_turned(i + 1, 1 - b)
                            act.wait_ge(qk_ready, g + 1)
                            if later(g - NU + 1):
                                act.wait_ge(terms, g - NU + 1)
                            nc.scalar.activation(swapped[0:HP, n], qb[HP:P, n], ACT.Copy)
                            nc.scalar.activation(swapped[HP:P, n], qb[0:HP, n], ACT.Copy).then_inc(swap_ready, 1)
                            if later(g):
                                high(g - 1, (n - 1) % NU)
                            if later(g - 1):
                                middle(g - 2, (n - 2) % NU)

                copy_turned(0, 0)
                ends_apart(act, NC // 2, pair)
                high(NC * NU - 1, NU - 1)
                middle(NC * NU - 2, NU - 2)
                middle(NC * NU - 1, NU - 1)

            @block.gpsimd
            def _(pool):
                def what_hi_leaves(g, n):
                    pool.wait_ge(hi_ready, g + 1)
                    if later(g - NU + 1):
                        pool.wait_ge(lo_ready, g - NU + 1)
                    nc.gpsimd.tensor_tensor(rest[:, n], roped[:, n], parts[:, n, 0],
                                            ALU.subtract).then_inc(rest_ready, 1)

                def chunk(i, first, last_chunk):
                    for n in range(NU):
                        g = i * NU + n
                        pool.wait_ge(terms, g + 1)
                        if later(g - NU + 1):
                            pool.wait_ge(rest_ready, g - NU + 1)
                        nc.gpsimd.tensor_tensor(roped[:, n], term[:, n, 0], term[:, n, 1],
                                                ALU.add).then_inc(roped_ready, 1)
                        if later(g):
                            what_hi_leaves(g - 1, (n - 1) % NU)

                ends_apart(pool, NC, chunk)
                what_hi_leaves(NC * NU - 1, NU - 1)

            @block.vector
            def _(dve):
                def normalise(i, b):
                    if later(i - 1):
                        dve.wait_ge(t_ready, i - 1)
                    for k in range(TPC):
                        t = i * TPC + k
                        last = nc.vector.tensor_scalar(xn[:, b, k, :], mem.x[:, t, :], mem.mv[:, t, 0:1],
                                                       mem.rstd[:, t, 0:1], ALU.subtract, ALU.mult)
                    last.then_inc(xn_ready, 1)

                def low(g, n):
                    dve.wait_ge(mid_ready, g + 1)
                    nc.vector.tensor_tensor(parts[:, n, 2], rest[:, n], parts[:, n, 1], ALU.subtract).then_inc(lo_ready, 1)

                def pair(p, first, last_pair):
                    for b in range(2):
                        i = 2 * p + b
                        if not last_pair:
                            normalise(i + 2, b)
                        if b == 0:
                            dve.wait_ge(trig_here, p + 1)
                        dve.wait_ge(v_ready, i + 1)
                        for k in range(TPC):
                            last = nc.vector.tensor_tensor(mem.v[:, i * TPC + k, :], vb[:, k, :], b_v[:], ALU.add)
                        last.then_inc(v_read, 1)
                        for n in range(NU):
                            a, h, g = n // DH, n % DH, i * NU + n
                            dve.wait_ge(swap_ready, g + 1)
                            if later(g - NU + 1):
                                dve.wait_ge(roped_ready, g - NU + 1)
                            nc.vector.scalar_tensor_tensor(term[:, n, 0], qb[:, n], b_qk[:, 0, a, h:h + 1],
                                                           trig[:, 0, bass.ts(i, CH)], ALU.add, ALU.mult)
                            nc.vector.scalar_tensor_tensor(term[:, n, 1], swapped[:, n], b_qk[:, 1, a, h:h + 1],
                                                           trig[:, 1, bass.ts(i, CH)], ALU.add,
                                                           ALU.mult).then_inc(terms, 1)
                            if later(g - 1):
                                low(g - 2, (n - 2) % NU)

                aggregate_stats(nc, mem, stats_done)
                dve.wait_ge(std_ready, 1)
                nc.vector.reciprocal(mem.rstd[:], std[:]).then_inc(rstd_ready, 1)
                dve.wait_ge(rstd_ready, 1)
                normalise(0, 0)
                normalise(1, 1)
                dve.wait_ge(loaded, 80)
                ends_apart(dve, NC // 2, pair)
                low(NC * NU - 2, NU - 2)
                low(NC * NU - 1, NU - 1)

            @block.tensor
            def _(pe):
                def turn(i, b):
                    pe.wait_ge(xn_ready, i + 1)
                    for h in range(DH):
                        for k in range(TPC):
                            last = nc.tensor.transpose(tp[:, h, k * P:(k + 1) * P], xn[:, b, k, h * P:(h + 1) * P],
                                                       mem.ident[:])
                    last.then_inc(t_ready, 1)

                def pair(p, first, last_pair):
                    for b in range(2):
                        i = 2 * p + b
                        pe.wait_ge(xnt_ready, i + 1)
                        if later(i):
                            pe.wait_ge(v_read, i)
                        for k in range(TPC):
                            for h in range(DH):
                                last = nc.tensor.matmul(vb[:, k, :], xnt[:, b, h, k * P:(k + 1) * P], w_v[:, h, :],
                                                        start=(h == 0), stop=(h == DH - 1))
                        last.then_inc(v_ready, 1)
                        for n in range(NU):
                            a, half, g = n // DH, n % DH, i * NU + n
                            if later(g - NU + 1):
                                pe.wait_ge(terms, g - NU + 1)
                            for h in range(DH):
                                last = nc.tensor.matmul(qb[:, n, :], w_qk[:, a, h, half * P:(half + 1) * P],
                                                        xnt[:, b, h, :], start=(h == 0), stop=(h == DH - 1))
                            last.then_inc(qk_ready, 1)
                            if n == 0 and not (last_pair and b == 1):
                                turn(i + 1, 1 - b)

                turn(0, 0)
                pe.wait_ge(loaded, 80)
                ends_apart(pe, NC // 2, pair)


def attention(nc, mem):
    with ExitStack() as ctx:
        def sb(name, shape, dt):
            return ctx.enter_context(nc.sbuf_tensor(name, shape, dt))

        q_rows = sb("q_rows", [P, 2, S], BF16)
        k_rows = sb("k_rows", [P, 2, S], BF16)
        v_ones = sb("v_ones", [P, 2, NKT, VW], F32)
        prob = sb("prob", [P, PBUF, QH], F32)
        tile_max = prob[:].rearrange("p b (t q) -> p (b t) q", q=CH)
        max_copy = sb("max_copy", [P, 2, CH], F32)
        acc_sb = sb("acc_sb", [P, 2, CH], F32)
        part_max = sb("part_max", [P, QT, NC], F32)
        neg_max = sb("neg_max", [P, QT], F32)
        neg_rest = sb("neg_rest", [P, QT], F32)
        neg_parts = sb("neg_parts", [P, NPART, NT], BF16)
        max_rows = sb("max_rows", [NPART * NT, P], BF16)
        sc = ctx.enter_context(nc.psum_tensor("scores", [P, SB, CH], F32))
        acc = ctx.enter_context(nc.psum_tensor("acc", [P, CH], F32))
        mx = ctx.enter_context(nc.psum_tensor("max_scores", [P, 2, 2, CH], F32))
        (rows_loaded, ones_set, v_ready, max_ready, max_read, neg_ready, max_copied, max_moved, passed, first_ready, copy_ready,
         s_ready, exp_done, pv_done, acc_read, split_step, stored0, stored1) = make_sems(
            nc, ctx, "at", "rows ones v maxready maxread neg maxcopied maxmoved passed firstready copyready s exp pv accread "
            "split stored0 stored1")
        stored = (stored0, stored1)
        LOAD = 16 * 2 * 2 * len(Q_SLOTS)

        def pair_slot(h, half, m):
            if isinstance(h, int) and (h, half) == (0, 0):
                return m + 1
            return (2 * h + half) * SLOTS + m + (1 if m >= TURN_AT else 0)

        def pair_bank(h, half, m):
            if isinstance(h, int) and (h, half) == (0, 0):
                return (m + 1) % 2
            return (half * SLOTS + m + (1 if m >= TURN_AT else 0)) % 2

        def turn_slot(h, half, last):
            return (2 * h + half + 1) * SLOTS + (0 if last else TURN_AT)

        def turned(half, last):
            bank = ((half + 1) * SLOTS + (0 if last else TURN_AT)) % 2
            return mx[:, bank, 0, :].bitcast(BF16)[0:NPART * NT, 0:P]

        def load_rows(eng, rows, which, slots, h, par):
            for n, part in enumerate(slots):
                for s in range(2):
                    eng.dma_start(rows[n * DK + s * DK // 2:n * DK + (s + 1) * DK // 2, par, :],
                                  mem.qk_parts[which, part, s, bass.ds(h * (DK // 2), DK // 2), :]
                                  ).then_inc(rows_loaded, 16)

        def heads(eng, body):
            body(0, 0, True, False)
            with eng.Fori(0, (H - 2) // 2) as pair:
                body(2 * pair + 1, 1, False, False)
                body(2 * pair + 2, 0, False, False)
            body(H - 1, 1, False, True)

        with nc.Block() as block:
            @block.sync
            def _(sp):
                def load(h, par):
                    load_rows(sp, q_rows, 0, Q_SLOTS, h, par)
                    load_rows(sp, k_rows, 1, K_SLOTS, h, par)

                def store(h, half):
                    wait_apart(sp, acc_read, 2 * h + half + 1, passed)
                    for j in range(4):
                        sp.dma_start(mem.att_t[bass.ds(h * DK, DK), half * QH + j * CH:half * QH + (j + 1) * CH],
                                     acc_sb[32 * j:32 * j + DK, half, :]).then_inc(stored[half], 16)
                    sp.dma_start(mem.sums[bass.ds(h * NC + half * 4, 4), :],
                                 acc_sb[DK:DK + 97:32, half, :]).then_inc(stored[half], 16)

                def move_max(h, half, par):
                    sp.wait_ge(max_copied, 2 * h + half + 1)
                    for n in range(NPART):
                        sp.dma_start(q_rows[KR + n:KR + n + 1, par, half * QH:(half + 1) * QH]
                                     .rearrange("o (t q) -> o t q", q=P),
                                     max_rows[n * NT + half * QT:n * NT + (half + 1) * QT, :]).then_inc(max_moved, 16)

                def head(h, par, first, last):
                    if not last:
                        if first:
                            sp.wait_ge(max_ready, 2)
                        else:
                            sp.wait_ge(s_ready, h * (4 * STEPS))
                        load(h + 1, 1 - par)
                    if not first:
                        store(h - 1, 1)
                    move_max(h, 1, par)
                    store(h, 0)
                    if not last:
                        move_max(h + 1, 0, 1 - par)

                load_rows(sp, q_rows, 0, Q_SLOTS, 0, 0)
                move_max(0, 0, 0)
                heads(sp, head)
                store(H - 1, 1)
                for s in stored:
                    sp.wait_ge(s, 16 * 5 * H)

            @block.gpsimd
            def _(pool):
                nc.gpsimd.memset(v_ones[:], 1.0).then_inc(ones_set, 1)
                pool.wait_ge(ones_set, 1)
                nc.gpsimd.memset(k_rows[KR:P, :, :], 1.0).then_inc(ones_set, 1)
                pool.wait_ge(ones_set, 2)
                nc.gpsimd.memset(neg_parts[:], 0.0).then_inc(ones_set, 1)
                pool.wait_ge(ones_set, 3)

                def copy_v(h, par):
                    nc.gpsimd.tensor_copy(v_ones[:, par, :, 0:DK], mem.v[:, :, bass.ds(h * DK, DK)]).then_inc(v_ready, 1)

                copy_v(0, 0)
                copy_v(1, 1)
                with pool.Fori(0, (H - 2) // 2) as pair:
                    for par in range(2):
                        pool.wait_ge(pv_done, (2 * pair + par + 1) * STEPS)
                        copy_v(2 * pair + 2 + par, par)

            @block.tensor
            def _(pe):
                def max_unit(h, half, par, n, copied=False):
                    t, c = n // NC, n % NC
                    if n == 0 and half == 0:
                        pe.wait_ge(rows_loaded, (h + 1) * LOAD)
                    slot, m = pair_slot(h, half, n // 2), n // 2
                    if copied and n % 2 == 0:
                        if m >= 2:
                            pe.wait_ge(copy_ready, m - 1)
                    elif (copied or n % 2 == 0) and later(slot - 1):
                        pe.wait_ge(max_read, slot - 1)
                    q0 = (half * QT + t) * P
                    mm = nc.tensor.matmul(mx[:, pair_bank(h, half, n // 2), n % 2, :], q_rows[0:KR, par, q0:q0 + P],
                                          k_rows[0:KR, par, c * CH:(c + 1) * CH], start=True, stop=True)
                    if n % 2:
                        mm.then_inc(max_ready, 1)
                    elif copied:
                        mm.then_inc(first_ready, 1)

                def turn_max(h, half, last=False):
                    pe.wait_ge(max_read, turn_slot(h, half, last) - 1)
                    pe.wait_ge(neg_ready, 2 * h + half + 1)
                    nc.tensor.transpose(turned(half, last), neg_parts[:].rearrange("p s t -> p (s t)"),
                                        mem.ident_b[:]).then_inc(max_ready, 1)

                def max_stream(h, half, par, u, last_head):
                    nh, nhalf, npar = (h, 1, par) if half == 0 else (h + 1, 0, 1 - par)
                    if last_head and half == 1:
                        return
                    if u < MAXU:
                        max_unit(nh, nhalf, npar, u)
                    elif last_head:
                        if u == MAXU + 2 * TURN_AT:
                            turn_max(h, 1, last=True)
                    else:
                        if u == MAXU + 2 * TURN_AT:
                            turn_max(nh, nhalf)
                        max_unit(h + 1, half, 1 - par, u - MAXU)

                def scores(h, par, t, j):
                    half, kt, n = t // NKT, t % NKT, 4 * t + j
                    if kt == 0 and j == 0:
                        pe.wait_ge(max_moved, (2 * h + half + 1) * 16 * NPART)
                    ago = 1 if n == 0 else SB
                    done = h * (4 * STEPS) + n + 1 - ago
                    if later(done):
                        pe.wait_ge(exp_done, done)
                    q0 = half * QH + j * CH
                    nc.tensor.matmul(sc[:, n % SB, :], k_rows[0:KM, par, kt * P:(kt + 1) * P],
                                     q_rows[0:KM, par, q0:q0 + CH], start=True, stop=True).then_inc(s_ready, 1)

                def weigh(h, par, t):
                    half, kt = t // NKT, t % NKT
                    if t == 0:
                        pe.wait_ge(v_ready, h + 1)
                    if kt == 0 and later(2 * h + half):
                        pe.wait_ge(acc_read, 2 * h + half)
                    pe.wait_ge(exp_done, h * (4 * STEPS) + 4 * t + 4)
                    for i in range(4):
                        last = nc.tensor.matmul(acc[32 * i:32 * i + VW, :], v_ones[:, par, kt, :],
                                                prob[:, t % PBUF, i * CH:(i + 1) * CH], start=(kt == 0),
                                                stop=(kt == NKT - 1), tile_position=(0, 32 * i))
                    last.then_inc(pv_done, 1)

                def head(h, par, first, last_head):
                    for t in range(STEPS):
                        half, kt = t // NKT, t % NKT
                        for j in range(4):
                            if t < STEPS - 1:
                                scores(h, par, t + 1, j)
                            elif not last_head:
                                scores(h + 1, 1 - par, 0, j)
                            max_stream(h, half, par, LEAD + 4 * kt + j, last_head)
                            if j == 1:
                                if t > 0:
                                    weigh(h, par, t - 1)
                                elif not first:
                                    weigh(h - 1, 1 - par, STEPS - 1)

                pe.sem_inc(max_ready, 1)
                pe.wait_ge(ones_set, 3)
                for n in range(MAXU):
                    max_unit(0, 0, 0, n, copied=True)
                for n in range(LEAD):
                    if n == 2 * TURN_AT:
                        turn_max(0, 0)
                    max_unit(0, 1, 0, n)
                for j in range(4):
                    scores(0, 0, 0, j)
                heads(pe, head)
                weigh(H - 1, 1, STEPS - 1)

            @block.scalar
            def _(act):
                def copy_block(h, half):
                    act.wait_ge(pv_done, h * STEPS + (half + 1) * NKT)
                    if later(h):
                        act.wait_ge(stored[half], h * (16 * 5))
                    nc.scalar.activation(acc_sb[:, half, :], acc[:], ACT.Copy).then_inc(acc_read, 1)

                def head(h, par, first, last_head):
                    for t in range(STEPS):
                        if not (first and t < PBUF):
                            act.wait_ge(pv_done, h * STEPS + t - PBUF + 1)
                        for j in range(4):
                            n = 4 * t + j
                            act.wait_ge(s_ready, h * (4 * STEPS) + n + 1)
                            nc.scalar.activation(prob[:, t % PBUF, j * CH:(j + 1) * CH], sc[:, n % SB, :], ACT.Exp,
                                                 scale=SCALE).then_inc(exp_done, 1)
                        if t == 0 and not first:
                            copy_block(h - 1, 1)
                        if t == NKT:
                            copy_block(h, 0)

                load_rows(act, k_rows, 1, K_SLOTS, 0, 0)
                for m in range(MAXP):
                    act.wait_ge(first_ready, m + 1)
                    if m >= 2:
                        act.wait_ge(max_read, pair_slot(0, 0, m - 2) + 1)
                    nc.scalar.activation(max_copy[:, m % 2, :], mx[:, pair_bank(0, 0, m), 0, :],
                                         ACT.Copy).then_inc(copy_ready, 1)
                heads(act, head)
                copy_block(H - 1, 1)

            @block.vector
            def _(dve):
                def max_pairs(h, half, first, end):
                    for m in range(first, end):
                        t, c = 2 * m // NC, 2 * m % NC
                        dve.wait_ge(max_ready, pair_slot(h, half, m) + 1)
                        nc.vector.tensor_reduce(part_max[:, t, c:c + 2], mx[:, pair_bank(h, half, m), :, :], AXX,
                                                ALU.max).then_inc(max_read, 1)

                def first_pairs():
                    for m in range(MAXP):
                        t, n = m // (NC // 2), m % (NC // 2)
                        dve.wait_ge(copy_ready, m + 1)
                        dve.wait_ge(max_ready, pair_slot(0, 0, m) + 1)
                        if m:
                            dve.wait_ge(max_read, pair_slot(0, 0, m - 1) + 1)
                        out = tile_max[:, t, :] if n == NC // 2 - 1 else acc_sb[:, n % 2, :]
                        start = acc_sb[:, (n - 1) % 2, CH - 1:CH] if n else float(-np.finfo(np.float32).max)
                        nc.vector.tensor_tensor_scan(out, mx[:, pair_bank(0, 0, m), 1, :], max_copy[:, m % 2, :], start,
                                                     ALU.max, ALU.max).then_inc(max_read, 1)

                def split_max(h, half, scanned=False):
                    b, cols = 2 * h + half, slice(half * QT, (half + 1) * QT)
                    dve.wait_ge(max_read, pair_slot(h, half, MAXP - 1) + 1)
                    steps = Chain(dve, split_step, b * 4)
                    source = tile_max[:, :, CH - 1:CH] if scanned else part_max[:]
                    steps.link(nc.vector.tensor_reduce(neg_max[:], source, AXX, ALU.max, negate=True))
                    steps.link(nc.vector.tensor_copy(neg_parts[:, 0, cols], neg_max[:]))
                    steps.link(nc.vector.tensor_tensor(neg_rest[:], neg_max[:], neg_parts[:, 0, cols], ALU.subtract))
                    steps.link(nc.vector.tensor_copy(neg_parts[:, 1, cols], neg_rest[:]))
                    nc.vector.tensor_tensor(neg_parts[:, 2, cols], neg_rest[:], neg_parts[:, 1, cols],
                                            ALU.subtract).then_inc(neg_ready, 1)

                def copy_turned(h, half, last=False):
                    if later(2 * h + half):
                        dve.wait_ge(max_moved, (2 * h + half) * (16 * NPART))
                    dve.wait_ge(max_ready, turn_slot(h, half, last) + 1)
                    copy = nc.vector.tensor_copy(max_rows[:], turned(half, last))
                    copy.then_inc(max_copied, 1)
                    dve.wait_ge(max_copied, 2 * h + half + 1)
                    dve.sem_inc(max_read, 1)

                def head(h, par, first, last_head):
                    for half in range(1 if last_head else 2):
                        nh, nhalf = (h, 1) if half == 0 else (h + 1, 0)
                        max_pairs(nh, nhalf, LEAD // 2, MAXP)
                        split_max(nh, nhalf)
                        if last_head:
                            copy_turned(nh, nhalf, last=True)
                        else:
                            max_pairs(h + 1, half, 0, TURN_AT)
                            copy_turned(nh, nhalf)
                            max_pairs(h + 1, half, TURN_AT, LEAD // 2)

                dve.sem_inc(max_read, 1)
                dve.wait_ge(ones_set, 3)
                first_pairs()
                split_max(0, 0, scanned=True)
                max_pairs(0, 1, 0, TURN_AT)
                copy_turned(0, 0)
                max_pairs(0, 1, TURN_AT, LEAD // 2)
                heads(dve, head)


def attention_output(nc, mem, io):
    with ExitStack() as ctx:
        def sb(name, shape, dt):
            return ctx.enter_context(nc.sbuf_tensor(name, shape, dt))

        w_o = sb("w_o", [P, DH, D], F32)
        b_o = sb("b_o", [P, 1, D], F32)
        att = sb("att_all", [P, DH, S], F32)
        att_n = sb("att_norm", [P, 2, DH, CH], F32)
        sums = sb("sums_all", [P, CH], F32)
        recip = sb("sums_recip", [P, CH], F32)
        to_rows = sb("to_rows", [P, DH, NC, P], F32)
        bc = ctx.enter_context(nc.psum_tensor("recip_rows", [P, 2, DH, CH], F32))
        ob = ctx.enter_context(nc.psum_tensor("ao_out", [P, 2, TPC, D], F32))
        (loaded, sums_loaded, one_hot, bias_added, recip_ready, rows_ready, att_ready, o_ready, x_ready,
         dve_passed) = make_sems(
            nc, ctx, "ao", "loaded sumsloaded onehot bias recip rows att o x passed")
        att_loaded = make_sems(nc, ctx, "ao", " ".join(f"att{i}" for i in range(NC)))

        with nc.Block() as block:
            @block.sync
            def _(sp):
                sp.dma_start(sums[:], mem.sums).then_inc(sums_loaded, 16)
                for i in range(NC):
                    sp.dma_start(att[:, :, i * CH:(i + 1) * CH],
                                 mem.att_t[:, i * CH:(i + 1) * CH].rearrange("(h p) t -> p h t", p=P)).then_inc(att_loaded[i], 16)
                    if i == 0:
                        sp.dma_start(w_o[:], io.w_o.rearrange("(h p) o -> p h o", p=P)).then_inc(loaded, 16)
                        sp.dma_start(b_o[:, 0, :], io.b_o).then_inc(loaded, 16)

            @block.gpsimd
            def _(pool):
                nc.gpsimd.memset(to_rows[:], 0.0).then_inc(one_hot, 1)
                pool.wait_ge(one_hot, 1)
                v = to_rows[:].rearrange("p h c (a r) -> p h c a r", r=DK)
                nc.gpsimd.affine_select(out=v, in_=v, compare_op=ALU.not_equal, fill=1.0, base=0,
                                        pattern=[[-NC * H // DH, DH], [-1, NC], [-NC, H // DH], [0, DK]],
                                        channel_multiplier=1).then_inc(one_hot, 1)
                pool.wait_ge(loaded, 32)
                with pool.Fori(0, NC) as i:
                    xs = mem.x[:, bass.ts(i, TPC), :]
                    nc.gpsimd.tensor_tensor(xs, xs, b_o[:].to_broadcast([P, TPC, D]), ALU.add).then_inc(bias_added, 1)

            @block.tensor
            def _(pe):
                def rows(i):
                    if i >= 2:
                        pe.wait_ge(att_ready, i - 1)
                    for h in range(DH):
                        last = nc.tensor.matmul(bc[:, i % 2, h, :], to_rows[:, h, i, :], recip[:], start=True, stop=True)
                    last.then_inc(rows_ready, 1)

                pe.wait_ge(one_hot, 2)
                pe.wait_ge(recip_ready, 1)
                rows(0)
                pe.wait_ge(loaded, 32)
                for i in range(NC):
                    if i < NC - 1:
                        rows(i + 1)
                    pe.wait_ge(att_ready, i + 1)
                    if i >= 2:
                        pe.wait_ge(x_ready, i - 1)
                    for k in range(TPC):
                        for h in range(DH):
                            last = nc.tensor.matmul(ob[:, i % 2, k, :], att_n[:, i % 2, h, k * P:(k + 1) * P],
                                                    w_o[:, h, :], start=(h == 0), stop=(h == DH - 1))
                    last.then_inc(o_ready, 1)

            @block.vector
            def _(dve):
                def normalise(i):
                    dve.wait_ge(att_loaded[i], 16)
                    dve.wait_ge(rows_ready, i + 1)
                    if i >= 2:
                        dve.wait_ge(o_ready, i - 1)
                    nc.vector.tensor_tensor(att_n[:, i % 2], bc[:, i % 2], att[:, :, i * CH:(i + 1) * CH],
                                            ALU.mult).then_inc(att_ready, 1)

                dve.wait_ge(sums_loaded, 16)
                nc.vector.reciprocal(recip[:], sums[:]).then_inc(recip_ready, 1)
                normalise(0)
                for i in range(NC):
                    if i < NC - 1:
                        normalise(i + 1)
                    dve.wait_ge(bias_added, i + 1)
                    dve.wait_ge(o_ready, i + 1)
                    xs = mem.x[:, i * TPC:(i + 1) * TPC, :]
                    nc.vector.tensor_tensor(xs, ob[:, i % 2], xs, ALU.add).then_inc(x_ready, 1)


def hybrid_kernel(nc, io, out):
    with ExitStack() as ctx:
        def sb(name, shape, dt, where=ctx):
            return where.enter_context(nc.sbuf_tensor(name, shape, dt))

        mem = Mem()
        mem.x = sb("x_res", [P, NT, D], F32)
        mem.six = sb("bn_six", [P, NT, 6], F32)
        mem.mv = sb("mean_var", [P, NT, 2], F32)
        mem.rstd = sb("rstd", [P, NT, 1], F32)
        mem.ident = sb("ident", [P, P], F32)
        mem.ident_b = sb("ident_b", [P, P], BF16)
        mem.eps = sb("eps", [P, 1], F32)
        mem.w_ffn = sb("w_ffn", [P, DH, 2 * D], F32)
        with ExitStack() as scan:
            mem.xp = sb("x_parts", [P, NPART, DH, S], BF16, scan)
            mem.b_rep = sb("b_rep", [P, S], F32, scan)
            mem.c_rep = sb("c_rep", [P, S], F32, scan)
            mem.delta = sb("delta", [P, S], F32, scan)
            mem.a_scale = sb("a_scale", [P, NJ], F32, scan)
            mem.spread = sb("spread", [P, NJH, P], BF16, scan)
            mem.gather = sb("gather", [P, NJ, 32], F32, scan)
            mem.carry = sb("carry", [P, NJ], F32, scan)
            norm_and_project(nc, mem, io)
            selective_scan(nc, mem)
        ffn(nc, mem, "f1")
        mem.qk_parts = nc.dram_tensor("qk_parts", [2, NPART, 2, D // 2, S], BF16, kind="Internal").ap()
        attn = ExitStack()
        mem.v = sb("v_all", [P, NKT, D], F32, attn)
        attention_project(nc, mem, io)
        mem.att_t = nc.dram_tensor("att_t", [D, S], F32, kind="Internal").ap()
        mem.sums = nc.dram_tensor("att_sums", [H * NC, CH], F32, kind="Internal").ap()
        attention(nc, mem)
        attn.close()
        attention_output(nc, mem, io)
        ffn(nc, mem, "f2", out)


def rope_tables():
    freq = (1.0 / np.float32(10000.0) ** (np.arange(0, DK, 2, dtype=np.float32) / np.float32(DK))).astype(np.float32)
    ang = (np.arange(S, dtype=np.float32)[None, :] * freq[:, None]).astype(np.float32)
    cos, sin = np.tile(np.cos(ang), (P // DK, 1)), np.tile(np.sin(ang), (P // DK, 1))
    return np.stack([np.concatenate([cos, cos]), np.concatenate([-sin, sin])]).astype(np.float32)


def kernel(**inputs):
    import concourse.bacc as bacc
    from concourse.bass_utils import run_bass_kernel_spmd

    a = {n.removeprefix("L0_"): np.asarray(v) for n, v in inputs.items()}
    halves = lambda w: w.reshape(*w.shape[:-1], DH, P // DK, 2, DK // 2).swapaxes(-3, -2)
    by_halves = lambda w: halves(w).reshape(w.shape)
    swap = lambda w: halves(w)[..., ::-1, :, :].reshape(w.shape)
    by_state = lambda w: np.tile(w.T, (1, CPT))
    arrays = {
        "x": a["attn_a_sequence"],
        "a_tiles": a["attn_a_A"].reshape(NJ, P).T,
        "w_bcd": np.stack([by_state(a["attn_a_W_B"]), by_state(a["attn_a_W_C"]),
                           np.tile(a["attn_a_W_Delta"].T, (1, P))], axis=1),
        "bias_bcd": np.stack([np.tile(a["attn_a_b_B"], CPT), np.tile(a["attn_a_b_C"], CPT),
                              np.tile(a["attn_a_b_Delta"], P), np.tile(a["attn_a_bias_Delta"], P)], axis=1),
        "theta": a["ffn_theta"], "theta_noise": a["ffn_theta_noise"],
        "phi": a["ffn_phi"], "phi_noise": a["ffn_phi_noise"],
        "w_qk": np.stack([by_halves(w) for w in (a["attn_b_Wq"], a["attn_b_Wk"])]),
        "b_qk": np.stack([np.stack([order(b) for b in (a["attn_b_bq"], a["attn_b_bk"])]) for order in (by_halves, swap)])
        .reshape(2, 2, DH, P).transpose(3, 0, 1, 2),
        "w_v": a["attn_b_Wv"], "b_v": np.tile(a["attn_b_bv"], (P, 1)),
        "w_o": a["attn_b_Wo"], "b_o": np.tile(a["attn_b_bo"], (P, 1)),
        "trig": rope_tables(),
    }
    nc = bacc.Bacc("TRN2", target_bir_lowering=False, num_devices=1)
    io = Mem()
    arrays = {f"in_{name}": np.ascontiguousarray(value) for name, value in arrays.items()}
    for name, value in arrays.items():
        io.__dict__[name.removeprefix("in_")] = nc.dram_tensor(name, value.shape, F32, kind="ExternalInput").ap()
    out = nc.dram_tensor("out", (1, S, D), F32, kind="ExternalOutput").ap()
    hybrid_kernel(nc, io, out)
    r = run_bass_kernel_spmd(nc, [arrays], core_ids=[0])
    return r.results[0]["out"]
```
